# Optimizing a Trainium2 kernel written in Bass

```python
import numpy as np
import jax
import jax.numpy as jnp

def _softmax(x, axis=-1):
    return jax.nn.softmax(x, axis=axis)

def _gelu(x):
    return jax.nn.gelu(x, approximate=True)

def _silu(x):
    return jax.nn.silu(x)

def _sigmoid(x):
    return jax.nn.sigmoid(x)

def _layernorm(x, axis=-1, eps=1e-05):
    m = jnp.mean(x, axis=axis, keepdims=True)
    v = jnp.var(x, axis=axis, keepdims=True)
    return (x - m) / jnp.sqrt(v + eps)

def _scatter_add(tgt, idx, src, axis=0):
    return tgt.at[idx].add(src)

def _segment_sum(src, seg, n):
    return jax.ops.segment_sum(src, seg, n)
kernel_name = 'mk_vit_tower_cls_d1_tok_img256_r4_c1bb29'

def setup_inputs(seed: int=0):
    np.random.seed(seed)
    _w = jnp.asarray

    def _rec_inputs():
        import jax
        import jax.numpy as jnp
        _rk = jax.random.key(seed)
        x = -7.10856e-05 + 0.999911 * jax.random.normal(jax.random.fold_in(_rk, 1), (4, 64, 128, 64), jnp.float32)
        cls_tok = 0.02 * jax.random.normal(jax.random.fold_in(_rk, 5), (1, 1, 64), jnp.float32)
        return (x, cls_tok)
    x, cls_tok = _rec_inputs()

    def _L0_tok_setup():
        import jax, jax.numpy as jnp
        import numpy as np
        PATCH_LEN = 16
        STRIDE = 8
        PAD = 8
        key = jax.random.key(seed)
        k1, k2 = jax.random.split(key)
        x = jax.random.normal(k1, (32, 64, 128, 64), dtype=jnp.float32)
        in_feat = 64 * (PATCH_LEN // 2 + 1) * 2
        W = jax.random.normal(k2, (64, in_feat), dtype=jnp.float32) * 0.02
        return {'x': x, 'W': W}
    _L0_tok_all = _L0_tok_setup()
    _L0_tok_in = {k: v for k, v in _L0_tok_all.items() if k in ('W',)}
    del _L0_tok_all

    def _L0_attn_setup():
        import jax, jax.numpy as jnp
        import numpy as np
        B, T, C = (16, 512, 64)
        TT = T
        LAYER_ID, N_LAYER = (3, 6)
        key = jax.random.key(seed)
        ks = jax.random.split(key, 6)
        ratio_0_to_1 = LAYER_ID / (N_LAYER - 1)
        ratio_1_to_almost0 = 1.0 - LAYER_ID / N_LAYER
        h = np.arange(TT, dtype=np.float32)
        decay_speed = -5.0 + 8.0 * (h / (TT - 1)) ** (0.7 + 1.3 * ratio_0_to_1)
        curve = -(TT - 1 - h)
        time_w = jnp.asarray(np.exp(np.clip(curve * decay_speed, -30.0, 0.0)), dtype=jnp.float32)
        i = np.arange(C, dtype=np.float32) / C
        time_mix_k = jnp.asarray((i ** ratio_1_to_almost0).reshape(1, 1, C), dtype=jnp.float32)
        time_mix_v = jnp.asarray((i ** ratio_1_to_almost0 + 0.3 * ratio_0_to_1).reshape(1, 1, C), dtype=jnp.float32)
        time_mix_r = jnp.asarray((i ** (0.5 * ratio_1_to_almost0)).reshape(1, 1, C), dtype=jnp.float32)
        x = jax.random.normal(ks[0], (B, T, C), dtype=jnp.float32)
        scale = 0.02
        Wk = scale * jax.random.normal(ks[1], (C, C), dtype=jnp.float32)
        Wv = scale * jax.random.normal(ks[2], (C, C), dtype=jnp.float32)
        Wr = scale * jax.random.normal(ks[3], (C, C), dtype=jnp.float32)
        Wo = scale * jax.random.normal(ks[4], (C, C), dtype=jnp.float32)
        return {'x': x, 'time_w': time_w, 'time_mix_k': time_mix_k, 'time_mix_v': time_mix_v, 'time_mix_r': time_mix_r, 'Wk': Wk, 'Wv': Wv, 'Wr': Wr, 'Wo': Wo}
    _L0_attn_all = _L0_attn_setup()
    _L0_attn_in = {k: v for k, v in _L0_attn_all.items() if k in ('time_w', 'time_mix_k', 'time_mix_v', 'time_mix_r', 'Wk', 'Wv', 'Wr', 'Wo')}
    del _L0_attn_all

    def _L0_ffn_setup():
        import jax, jax.numpy as jnp
        import numpy as np
        B, S, H, F, E, K = (8, 1024, 64, 128, 16, 2)
        EPS = 1e-05
        key = jax.random.key(seed)
        ks = jax.random.split(key, 9)
        sc = 0.02
        return {'x': jax.random.normal(ks[0], (B, S, H), dtype=jnp.float32), 'gate_w': jax.random.normal(ks[1], (H, E), dtype=jnp.float32) * sc, 'gate_b': jnp.zeros((E,), dtype=jnp.float32), 'w1': jax.random.normal(ks[2], (E, H, F), dtype=jnp.float32) * sc, 'b1': jnp.zeros((E, F), dtype=jnp.float32), 'w2': jax.random.normal(ks[3], (E, F, H), dtype=jnp.float32) * sc, 'b2': jnp.zeros((E, H), dtype=jnp.float32), 'gamma': jnp.ones((H,), dtype=jnp.float32), 'beta': jnp.zeros((H,), dtype=jnp.float32)}
    _L0_ffn_all = _L0_ffn_setup()
    _L0_ffn_in = {k: v for k, v in _L0_ffn_all.items() if k in ('gate_w', 'gate_b', 'w1', 'b1', 'w2', 'b2', 'gamma', 'beta')}
    del _L0_ffn_all
    return {'x': x, 'cls_tok': cls_tok, 'L0_tok_W': _L0_tok_in['W'], 'L0_attn_time_w': _L0_attn_in['time_w'], 'L0_attn_time_mix_k': _L0_attn_in['time_mix_k'], 'L0_attn_time_mix_v': _L0_attn_in['time_mix_v'], 'L0_attn_time_mix_r': _L0_attn_in['time_mix_r'], 'L0_attn_Wk': _L0_attn_in['Wk'], 'L0_attn_Wv': _L0_attn_in['Wv'], 'L0_attn_Wr': _L0_attn_in['Wr'], 'L0_attn_Wo': _L0_attn_in['Wo'], 'L0_ffn_gate_w': _L0_ffn_in['gate_w'], 'L0_ffn_gate_b': _L0_ffn_in['gate_b'], 'L0_ffn_w1': _L0_ffn_in['w1'], 'L0_ffn_b1': _L0_ffn_in['b1'], 'L0_ffn_w2': _L0_ffn_in['w2'], 'L0_ffn_b2': _L0_ffn_in['b2'], 'L0_ffn_gamma': _L0_ffn_in['gamma'], 'L0_ffn_beta': _L0_ffn_in['beta']}

def reference(x, cls_tok, L0_tok_W, L0_attn_time_w, L0_attn_time_mix_k, L0_attn_time_mix_v, L0_attn_time_mix_r, L0_attn_Wk, L0_attn_Wv, L0_attn_Wr, L0_attn_Wo, L0_ffn_gate_w, L0_ffn_gate_b, L0_ffn_w1, L0_ffn_b1, L0_ffn_w2, L0_ffn_b2, L0_ffn_gamma, L0_ffn_beta):
    import jax
    import jax.numpy as jnp

    def _L0_tok_ref(x, W):
        import jax, jax.numpy as jnp
        import numpy as np
        PATCH_LEN = 16
        STRIDE = 8
        PAD = 8
        B, C, T, V = x.shape
        xp = jnp.pad(x, ((0, 0), (0, 0), (0, PAD), (0, 0)), mode='edge')
        Tp = T + PAD
        N = (Tp - PATCH_LEN) // STRIDE + 1
        idx = jnp.arange(N)[:, None] * STRIDE + jnp.arange(PATCH_LEN)[None, :]
        patches = xp[:, :, idx, :]
        patches = jnp.transpose(patches, (0, 4, 2, 3, 1))
        xf = jnp.fft.rfft(patches, axis=-2, norm='ortho')
        F = xf.shape[-2]
        x_real = xf.real.reshape(B, V, N, F * C)
        x_imag = xf.imag.reshape(B, V, N, F * C)
        x_emb = jnp.concatenate([x_real, x_imag], axis=-1)
        x_emb = x_emb @ W.T
        return x_emb.reshape(B, V * N, -1)

    def _L0_attn_ref(x, time_w, time_mix_k, time_mix_v, time_mix_r, Wk, Wv, Wr, Wo):
        import jax, jax.numpy as jnp
        import numpy as np
        B, T, C = (16, 512, 64)
        TT = T
        LAYER_ID, N_LAYER = (3, 6)
        Bx, Tx, Cx = x.shape
        maxlen = time_w.shape[0]
        xx = jnp.pad(x, ((0, 0), (1, 0), (0, 0)))[:, :-1]
        xk = x * time_mix_k + xx * (1.0 - time_mix_k)
        xv = x * time_mix_v + xx * (1.0 - time_mix_v)
        xr = x * time_mix_r + xx * (1.0 - time_mix_r)
        k = jnp.exp(jnp.clip(xk @ Wk, -60.0, 30.0))
        v = xv @ Wv
        r = xr @ Wr
        sum_k = jnp.cumsum(k, axis=1)
        kv = k * v
        t_idx = jnp.arange(Tx)
        d = t_idx[:, None] - t_idx[None, :]
        W = jnp.where(d >= 0, time_w[jnp.clip(maxlen - 1 - d, 0, maxlen - 1)], 0.0)
        wkv = jnp.einsum('tu,buc->btc', W, kv)
        rwkv = jax.nn.sigmoid(r) * wkv / sum_k
        return rwkv @ Wo

    def _L0_ffn_ref(x, gate_w, gate_b, w1, b1, w2, b2, gamma, beta):
        import jax, jax.numpy as jnp
        import numpy as np
        B, S, H, F, E, K = (8, 1024, 64, 128, 16, 2)
        EPS = 1e-05
        gate_logits = x @ gate_w + gate_b
        topk_vals, topk_idx = jax.lax.top_k(gate_logits, K)
        topk_w = jax.nn.softmax(topk_vals, axis=-1)
        h = jax.nn.relu(jnp.einsum('bsh,ehf->bsef', x, w1) + b1)
        expert_out = jnp.einsum('bsef,efh->bseh', h, w2) + b2
        sel = jnp.take_along_axis(expert_out, topk_idx[:, :, :, None], axis=2)
        moe = jnp.sum(topk_w[..., None] * sel, axis=2)
        y = x + moe
        mu = jnp.mean(y, axis=-1, keepdims=True)
        var = jnp.var(y, axis=-1, keepdims=True)
        return (y - mu) / jnp.sqrt(var + EPS) * gamma + beta
    h = _L0_tok_ref(x, L0_tok_W)
    h = jnp.concatenate([jnp.broadcast_to(cls_tok, (h.shape[0], 1, h.shape[2])), h], axis=1)
    h = h + _L0_attn_ref(_layernorm(h, axis=-1), L0_attn_time_w, L0_attn_time_mix_k, L0_attn_time_mix_v, L0_attn_time_mix_r, L0_attn_Wk, L0_attn_Wv, L0_attn_Wr, L0_attn_Wo)
    h = h + _L0_ffn_ref(_layernorm(h, axis=-1), L0_ffn_gate_w, L0_ffn_gate_b, L0_ffn_w1, L0_ffn_b1, L0_ffn_w2, L0_ffn_b2, L0_ffn_gamma, L0_ffn_beta)
    return h

_drawn_inputs = setup_inputs


def setup_inputs(seed=0):
    import zlib

    import numpy as np

    out = dict(_drawn_inputs(seed))
    spreads = {'L0_ffn_gate_b': (0.0, 0.446),
     'L0_ffn_b1': (0.0, 2.0),
     'L0_ffn_b2': (0.0, 0.8),
     'L0_ffn_gamma': (1.0, 0.6),
     'L0_ffn_beta': (0.0, 0.8)}
    factors = {'L0_attn_time_w': 8.0,
     'L0_attn_time_mix_k': 8.0,
     'L0_attn_time_mix_v': 8.0,
     'L0_attn_time_mix_r': 8.0,
     'L0_attn_Wk': 8.0,
     'L0_attn_Wv': 4.96,
     'L0_attn_Wr': 8.0,
     'L0_attn_Wo': 6.107,
     'L0_ffn_w1': 24.074,
     'L0_ffn_w2': 12.075,
     'L0_ffn_gate_w': 3.358}
    for name, (base, spread) in spreads.items():
        noise = np.random.default_rng([zlib.crc32(name.encode()), seed]).standard_normal(out[name].shape)
        drawn = base * np.exp(spread * noise) if base else spread * noise
        out[name] = jnp.asarray(drawn.astype(out[name].dtype))
    for name, factor in factors.items():
        out[name] = (out[name] * factor).astype(out[name].dtype)
    return out
```

```python
from contextlib import ExitStack

import concourse.bass as bass
from concourse import mybir

F32 = mybir.dt.float32
F32R = mybir.dt.float32r
BF16 = mybir.dt.bfloat16
U32 = mybir.dt.uint32
ALU = mybir.AluOpType
ACT = mybir.ActivationFunctionType
AX_X = mybir.AxisListType.X

P = 128
D = 64
NB = 4
VARS = 64
NPATCH = 16
TOK = VARS * NPATCH
NT = TOK // P
HALF = TOK // 2
NE = 16
NPAIR = NE // 2
FF = 128
STEPS = 2 * NPAIR
WLEN = 512
KPAD = 1024
EPS = 1e-5
PARTS = 3
C_ID, C_DUP, C_I3, C_DFT, C_END = 0, 128, 192, 208, 224


def build(nc, x, cls_tok, tok_W, time_w, mix_k, mix_v, mix_r, Wk, Wv, Wr, Wo,
          gate_w, gate_b, w1, b1, w2, b2, gamma, beta, consts, scratch, out):
    with ExitStack() as ctx:
        def sb(name, shape, dt=F32):
            return ctx.enter_context(nc.sbuf_tensor(name, shape, dt))

        def psum(name, shape, dt=F32):
            return ctx.enter_context(nc.psum_tensor(name, shape, dt))

        def sem(name):
            return ctx.enter_context(nc.semaphore(name))

        cst = sb("cst", [P, C_END])
        ident = cst[:, C_ID:C_ID + P]
        dup2 = cst[:, C_DUP:C_DUP + D]
        identb = sb("identb", [P, P], BF16)
        sel = sb("sel", [P, NE, P], BF16)
        iota = sb("iota", [P, NE])
        ones = sb("ones", [P, HALF])
        spare = sb("spare", [P, 8])
        mhalf = sb("mhalf", [P, NT])
        kept = sb("kept", [P, 2, NB, NT, D])
        wt18 = kept[0:18, :, :, :, :].rearrange("k a b t d -> k (a b t) d")
        wfp = sb("wfp", [16, D, D])
        wf = sb("wf", [P, 4, 2, D])
        wraw = sb("wraw", [P, 3, D])
        mixf = sb("mixf", [P, 3])
        wmix = sb("wmix", [P, 3, D])
        wobd = sb("wobd", [P, P])
        twrow = sb("twrow", [1, WLEN])
        padrow = sb("padrow", [1, KPAD + P])
        grev = sb("grev", [P, KPAD + 1])
        G = sb("G", [P, KPAD + 1])
        gw2 = sb("gw2", [P, NE])
        gbb = sb("gbb", [P, NE])
        gam = sb("gam", [P, D])
        bet = sb("bet", [P, D])
        w1raw = sb("w1raw", [P, NE, FF])
        w1h = sb("w1h", [P, NE, FF], F32R)
        w1l = sb("w1l", [P, NE, FF], F32R)
        w2s = sb("w2s", [P, NE, D])
        b1row = sb("b1row", [NE, FF])
        b1T = sb("b1T", [P, NE])
        b2x3 = sb("b2x3", [P, D])
        b2rem = sb("b2rem", [P, D])
        b2p = sb("b2p", [P, PARTS, D], BF16)

        xt = sb("xt", [P, 16, 4 * VARS])
        xpad = sb("xpad", [P, VARS])
        uv = sb("uv", [P, TOK])
        h = sb("h", [P, NT, D])
        xc = sb("xc", [P, NT, D])
        sq = sb("sq", [P, NT, D])
        stat = sb("stat", [P, 4, NT])
        x1 = sb("x1", [P, NT, 2, D])
        XX = sb("XX", [P, TOK + 1])
        kt = sb("kt", [P, NT, D])
        kv = sb("kv", [P, NT, D])
        kc = sb("kc", [P, HALF])
        sk = sb("sk", [P, HALF])
        kinit = sb("kinit", [P, 1])
        er = sb("er", [P, HALF])
        rq = sb("rq", [P, HALF])
        C0 = sb("C0", [P, HALF])
        wsum = sb("wsum", [P, HALF])
        rw = sb("rw", [P, HALF])
        x2s = sb("x2s", [P, NT, 2, D])
        xstk = sb("xstk", [P, TOK], F32R)
        lg = sb("lg", [P, NT, NE])
        top8 = sb("top8", [P, NT, 8])
        idx8 = sb("idx8", [P, NT, 8], U32)
        idxf = sb("idxf", [P, NT, 2])
        gsm = sb("gsm", [P, 4, NT])
        eq1 = sb("eq1", [P, NT, NE])
        eq2 = sb("eq2", [P, NT, NE])
        gw = sb("gw", [P, NT, NE])
        grem = sb("grem", [P, NT, NE])
        g3 = sb("g3", [P, NT, P], BF16)

        h1, x2 = kept[:, 0, :, :, :], kept[:, 1, :, :, :]
        xs = sb("xs", [P, NB, TOK], F32R)
        g3T = sb("g3T", [P, NB, TOK], BF16)

        hr = sb("hr", [P, 4, HALF])
        yT = sb("yT", [P, HALF])
        y3 = sb("y3", [P, 4, D])
        y3c = sb("y3c", [P, 4, D])
        y3q = sb("y3q", [P, 4, D])
        stat3 = sb("stat3", [P, 4, 4])
        yn = sb("yn", [P, 4, D])
        yg = sb("yg", [P, 4, D])
        fo = sb("fo", [P, 4, D])

        cl = sb("cl", [1, D])
        clw = sb("clw", [1, 3, D])
        cls4 = sb("cls4", [1, 4, 1])
        x1c = sb("x1c", [1, 2, D])
        XXc = sb("XXc", [P, 1])
        kv0t = sb("kv0t", [1, 2, D])
        k0 = sb("k0", [P, 1])
        c0s = sb("c0s", [P, 4])
        h1c = sb("h1c", [1, D])
        x2c = sb("x2c", [1, 2, D])
        x2cT = sb("x2cT", [P, 1])
        lgc = sb("lgc", [1, 1, NE])
        top8c = sb("top8c", [1, 1, 8])
        idx8c = sb("idx8c", [1, 1, 8], U32)
        idxfc = sb("idxfc", [1, 1, 2])
        gsmc = sb("gsmc", [1, 4, 1])
        eqc = sb("eqc", [1, 2, NE])
        gwc = sb("gwc", [1, 1, NE])
        gTc = sb("gTc", [NE, 1])
        gbc = sb("gbc", [P, NE])
        zc = sb("zc", [P, NE])
        hc = sb("hc", [P, NE])
        b2f = b2x3
        y3cl = sb("y3cl", [1, 4, D])

        A0 = psum("A0", [P, HALF])
        A1 = psum("A1", [P, HALF])
        A2 = psum("A2", [P, HALF])
        A0b = A0[:, :].bitcast(BF16)
        zb = psum("zb", [P, 2, HALF])
        gb = psum("gb", [P, 2, HALF])
        yb = psum("yb", [P, HALF])

        (l_cst, l_w18, l_wf, l_mix, l_wo, l_tw, l_scr, l_grev, l_gate, l_w1, l_w2, l_b, l_x, l_cls) = [
            sem("loaded_" + n) for n in ("consts", "tokw", "folded", "mix", "wo", "timew", "padrow", "grev",
                                         "gate", "w1", "w2", "bias", "x", "cls")]
        zeroed, ones_ok, cst_ready = sem("zeroed"), sem("ones_ok"), sem("cst_ready")
        fold_ps, fold_sb = sem("fold_ps"), sem("fold_sb")
        mixf_ok, wmix_ok = sem("mixf_ok"), sem("wmix_ok")
        pad_ok, G_ok = sem("pad_ok"), sem("G_ok")
        w1h_ok, w1l_ok, b1_ps, b1_ok, b2_ok = [sem(n) for n in ("w1h_ok", "w1l_ok", "b1_ps", "b1_ok", "b2_ok")]
        uv_ps, u_done, v_done, h_ps, h_done = [sem(n) for n in ("uv_ps", "u_done", "v_done", "h_ps", "h_done")]
        x1_ps, xx_lo, xx_hi = sem("x1_ps"), sem("xx_lo"), sem("xx_hi")
        kv_ps, kt_clip, kt_exp, kv_done = [sem(n) for n in ("kv_ps", "kt_clip", "kt_exp", "kv_done")]
        kc_ps, kc_clip, kc_exp, r_ps, er_done = [sem(n) for n in ("kc_ps", "kc_clip", "kc_exp", "r_ps", "er_done")]
        carry_ps, kinit_ok, sk_done, q_done, rq_done = [
            sem(n) for n in ("carry_ps", "kinit_ok", "sk_done", "q_done", "rq_done")]
        wkv_ps, wsum_done, rw_done, att_ps, h1_done = [
            sem(n) for n in ("wkv_ps", "wsum_done", "rw_done", "att_ps", "h1_done")]
        x2_kept, x2_ps, xs_hi, xs_lo, xs_kept = [sem(n) for n in ("x2_kept", "x2_ps", "xs_hi", "xs_lo", "xs_kept")]
        lg_ps, lg_done, top_done, idx_done = [sem(n) for n in ("lg_ps", "lg_done", "top_done", "idx_done")]
        idxf_done, gap_done, gexp, gden, g1_done, g2_done = [
            sem(n) for n in ("idxf_done", "gap_done", "gexp", "gden", "g1_done", "g2_done")]
        eq_done, eqg_done, gw_done = sem("eq_done"), sem("eqg_done"), sem("gw_done")
        gh_done, gr_done, gm_done, g3_done = [sem(n) for n in ("gh_done", "gr_done", "gm_done", "g3_done")]
        g3_ps, g3T_done, h1b_done = sem("g3_ps"), sem("g3T_done"), sem("h1b_done")
        z_ps, g_ps, relu_done, gated, h_used = [sem(n) for n in ("z_ps", "g_ps", "relu_done", "gated", "h_used")]
        y_ps, y_evac, moe_ps, moe_read = [sem(n) for n in ("y_ps", "y_evac", "moe_ps", "moe_read")]
        settled = sem("settled")
        yg_done, fo_done, stored = sem("yg_done"), sem("fo_done"), sem("stored")

        def ln_sems(tag):
            return {n: sem(f"{tag}_{n}") for n in ("sum", "center", "square", "sumsq", "var", "rstd", "out")}

        ln1, ln2, ln3, lnc = ln_sems("ln1"), ln_sems("ln2"), ln_sems("ln3"), ln_sems("lnc")
        c_xT, c_xx, c_kv, c_clip, c_exp, c_kv0, c_C0, c_C0sb, c_q, c_rw, c_att, c_h1, c_x2T, c_x2sb, c_lg = [
            sem("cls_" + n) for n in ("xT", "xx", "kv", "clip", "exp", "kv0", "C0", "C0sb", "q", "rw", "att", "h1",
                                      "x2T", "x2sb", "lg")]
        c_gate, c_gexp, c_g, c_gT, c_gTsb, c_z, c_zb, c_h, c_moe, c_y, c_fin, c_fo, c_out = [
            sem("cls_" + n) for n in ("gate", "gexp", "g", "gT", "gTsb", "z", "zb", "h", "moe", "y", "fin", "fo",
                                      "out")]

        uv_v = uv[:, :].rearrange("p (v n) -> p n v", n=NPATCH)

        def settle(eng, semaphore, value):
            eng.wait_ge(semaphore, value)
            eng.sem_inc(settled, 1)

        def ln_center(dve, s, n, src, st, dst, p, t):
            dve.tensor_reduce(st[0:p, 0, :], src, AX_X, ALU.add).then_inc(s["sum"], 1)
            dve.wait_ge(s["sum"], n + 1)
            mean = st[0:p, 0, :].unsqueeze(2).broadcast_to([p, t, D])
            dve.scalar_tensor_tensor(dst, mean, -1.0 / D, src, ALU.mult, ALU.add).then_inc(s["center"], 1)

        def ln_square(act, s, n, src, dst):
            act.wait_ge(s["center"], n + 1)
            act.activation(dst, src, ACT.Square).then_inc(s["square"], 1)

        def ln_var(dve, s, n, sqr, st, p):
            dve.wait_ge(s["square"], n + 1)
            dve.tensor_reduce(st[0:p, 1, :], sqr, AX_X, ALU.add).then_inc(s["sumsq"], 1)
            dve.wait_ge(s["sumsq"], n + 1)
            dve.tensor_scalar(st[0:p, 2, :], st[0:p, 1, :], 1.0 / D, EPS, ALU.mult, ALU.add).then_inc(s["var"], 1)

        def ln_rstd(pool, s, n, st, p, t):
            pool.wait_ge(s["var"], n + 1)
            pool.tensor_tensor(st[0:p, 3, :], st[0:p, 2, :], mhalf[0:p, 0:t], ALU.pow).then_inc(s["rstd"], 1)

        def ln_scale(dve, s, n, src, st, dsts, p, t):
            dve.wait_ge(s["rstd"], n + 1)
            r = st[0:p, 3, :].unsqueeze(2).broadcast_to([p, t, D])
            for dst in dsts:
                last = dve.tensor_tensor(dst, src, r, ALU.mult)
            last.then_inc(s["out"], 1)

        block = ctx.enter_context(nc.Block())

        @block.sync
        def _(sp):
            def load_x(b):
                for half in range(2):
                    src = x[b].rearrange("c (m h q) v -> h c m (q v)", h=2, q=4)[half]
                    sp.dma_start(xt[D * half:D * half + D, :, :], src).then_inc(l_x, 16)
                    sp.dma_start(xpad[D * half:D * half + D, :], x[b, :, 127, :]).then_inc(l_x, 16)

            def store(b, c):
                n = 2 * b + c
                sp.wait_ge(fo_done, n + 1)
                dst = out[b, 1 + c * HALF:1 + (c + 1) * HALF, :].rearrange("(i p) d -> p i d", p=P)
                sp.dma_start(dst, fo[:, :, :]).then_inc(stored, 16)

            sp.dma_start(cst[:, :], consts).then_inc(l_cst, 16)
            sp.dma_start(wt18[:, :, :], tok_W.rearrange("o (k c) -> k o c", c=D)).then_inc(l_w18, 16)
            sp.dma_start(twrow[:, :], time_w.rearrange("(a t) -> a t", a=1)).then_inc(l_tw, 16)
            sp.dma_start(cl[:, :], cls_tok[0]).then_inc(l_cls, 16)
            load_x(0)
            for half in range(2):
                rows = slice(D * half, D * half + D)
                for i, (w, m) in enumerate(((Wk, mix_k), (Wv, mix_v), (Wr, mix_r))):
                    sp.dma_start(wraw[rows, i, :], w).then_inc(l_mix, 16)
                    sp.dma_start(mixf[rows, i:i + 1], m[0].rearrange("a c -> c a")).then_inc(l_mix, 16)
            sp.wait_ge(fold_sb, 8)
            for half in range(2):
                for s in range(2):
                    p0 = 8 * s + 4 * half
                    for q in range(4):
                        sp.dma_start(wf[D * half:D * half + D, q, s, :],
                                     wfp[p0 + q:p0 + q + 1, :, :]).then_inc(l_wf, 16)
            sp.wait_ge(pad_ok, 3)
            sp.dma_start(scratch, padrow[:, :]).then_inc(l_scr, 16)
            sp.wait_ge(zeroed, 6)
            for half in range(2):
                rows = slice(D * half, D * half + D)
                sp.dma_start(wobd[rows, rows], Wo).then_inc(l_wo, 16)
                sp.dma_start(gw2[rows, :], gate_w).then_inc(l_gate, 16)
            sp.dma_start(gbb[:, :], gate_b.partition_broadcast(P)).then_inc(l_gate, 16)
            sp.dma_start(gam[:, :], gamma.partition_broadcast(P)).then_inc(l_gate, 16)
            sp.dma_start(bet[:, :], beta.partition_broadcast(P)).then_inc(l_gate, 16)
            sp.wait_ge(l_scr, 16)
            sp.dma_start(grev[:, :], bass.AP(scratch.tensor, 0, [[1, P], [1, KPAD + 1]])).then_inc(l_grev, 16)
            for half in range(2):
                sp.dma_start(w1raw[D * half:D * half + D, :, :], w1.rearrange("e i f -> i e f")).then_inc(l_w1, 16)
            sp.dma_start(w2s[:, :, :], w2.rearrange("e f o -> f e o")).then_inc(l_w2, 16)
            sp.dma_start(b1row[:, :], b1).then_inc(l_b, 16)
            for k in range(PARTS):
                sp.dma_start(b2x3[NE * k:NE * k + NE, :], b2).then_inc(l_b, 16)
            sp.wait_ge(uv_ps, 3)
            load_x(1)
            with sp.Fori(0, NB - 2) as b:
                sp.wait_ge(uv_ps, 3 * b + 6)
                load_x(b + 2)
                store(b, 0)
                store(b, 1)
            for b in range(NB - 2, NB):
                store(b, 0)
                store(b, 1)
            sp.wait_ge(c_fo, 1)
            for b in range(NB):
                sp.dma_start(out[b, 0:1, :], y3cl[:, 3, :]).then_inc(c_out, 16)
            sp.wait_ge(stored, 16 * (2 * NB + 1))
            sp.wait_ge(c_out, 16 * NB)

        @block.tensor
        def _(pe):
            mm = pe.matmul

            def embed(b, c):
                bank = (A0, A1)[c]
                for q in range(4):
                    last = mm(bank[:, :], wf[:, q, :, :], xt[:, 8 * c:8 * c + 8, VARS * q:VARS * q + VARS],
                              start=q == 0, stop=q == 3)
                last.then_inc(uv_ps, 1)

            def embed_edge(b):
                for q in range(4):
                    last = mm(A0[:, 0:VARS], wf[:, q, :, :], xpad[:, :], start=q == 0, stop=q == 3)
                last.then_inc(uv_ps, 1)

            def tokens(b):
                pe.wait_ge(v_done, 3 * b + 3)
                pe.wait_ge(u_done, 2 * b + 2)
                for i in range(NT):
                    last = mm(A1[:, D * i:D * i + D], uv[:, P * i:P * i + P], dup2, start=True, stop=True)
                last.then_inc(h_ps, 1)

            def turn(bank, src, c):
                for i in range(4):
                    last = pe.transpose(bank[:, P * i:P * i + P], src[:, 4 * c + i, :, :], ident)
                return last

            def kv_tokens(b, c):
                pe.wait_ge(xx_lo, 2 * b + c + 1)
                pe.wait_ge(xx_hi, 2 * b + c + 1)
                for i in range(4):
                    t = 4 * c + i
                    last = mm((A0, A1)[c][:, P * i:P * i + P], XX[:, P * t:P * t + P], wmix[:, 0:2, :],
                              start=True, stop=True)
                last.then_inc(kv_ps, 1)

            def channels(bank, i, done):
                for half in range(2):
                    last = mm(bank[D * half:D * half + D, :], wmix[:, i, :], XX[:, HALF * half:HALF * half + HALF],
                              start=True, stop=True)
                last.then_inc(done, 1)

            def stage_a(b, g):
                first = isinstance(b, int)
                if g == 0:
                    if not first:
                        pe.wait_ge(g3T_done, b)
                        pe.wait_ge(lg_done, b)
                    pe.wait_ge(l_x, 64 * b + 64)
                    embed(b, 0)
                elif g == 1:
                    embed(b, 1)
                    pe.wait_ge(u_done, 2 * b + 1)
                    pe.wait_ge(v_done, 3 * b + 1)
                    embed_edge(b)
                elif g == 2:
                    tokens(b)
                elif g == 4:
                    pe.wait_ge(ln1["out"], b + 1)
                    turn(A0, x1, 0).then_inc(x1_ps, 1)
                    turn(A1, x1, 1).then_inc(x1_ps, 1)
                elif g == 5:
                    kv_tokens(b, 0)
                    kv_tokens(b, 1)
                elif g == 6:
                    pe.wait_ge(kv_done, 2 * b + 1)
                    channels(A0, 0, kc_ps)
                    pe.wait_ge(kv_done, 2 * b + 2)
                    channels(A1, 2, r_ps)
                elif g == 7:
                    pe.wait_ge(kc_clip, b + 1)
                    for i in range(4):
                        last = mm(A0[D:P, 0:1], kt[:, i, :], ones[:, 0:1], start=i == 0, stop=i == 3)
                    last.then_inc(carry_ps, 1)
                elif g == 8:
                    pe.wait_ge(er_done, b + 1)
                    for i in range(4):
                        n = HALF - P * i
                        mm(A1[0:D, P * i:HALF], kv[:, i, :], G[:, 0:n], start=i == 0, stop=i == 3)
                        mm(A1[D:P, :], kv[:, i, :], G[:, n:n + HALF], start=i == 0, stop=False,
                           skip_group_check=True)
                    for i in range(4):
                        last = mm(A1[D:P, P * i:HALF], kv[:, 4 + i, :], G[:, 0:HALF - P * i], start=False,
                                  stop=i == 3, skip_group_check=True)
                    last.then_inc(wkv_ps, 1)
                elif g == 10:
                    pe.wait_ge(rw_done, b + 1)
                    pe.wait_ge(kinit_ok, b + 1)
                    for i in range(4):
                        last = mm(A0[:, P * i:P * i + P], rw[:, P * i:P * i + P], wobd[:, :], start=True, stop=True)
                    last.then_inc(att_ps, 1)
                elif g == 12:
                    pe.wait_ge(ln2["out"], b + 1)
                    turn(A1, x2s, 0).then_inc(x2_ps, 1)
                    turn(A0, x2s, 1).then_inc(x2_ps, 1)
                elif g == 13:
                    pe.wait_ge(xs_lo, 2 * b + 2)
                    for i in range(NT):
                        last = mm(A1[:, NE * i:NE * i + NE], xstk[:, P * i:P * i + P].bitcast(F32), gw2[:, :],
                                  start=True, stop=True)
                    last.then_inc(lg_ps, 1)
                elif g == 15:
                    pe.wait_ge(g3_done, b + 1)
                    for i in range(NT):
                        last = pe.transpose(A0b[:, P * i:P * i + P], g3[:, i, :], identb[:, :])
                    last.then_inc(g3_ps, 1)

            def expert_in(b, s):
                c, p = s // NPAIR, s % NPAIR
                for k in range(2):
                    e, n = 2 * p + k, 32 * b + 2 * s + k
                    moving = xs[:, b, HALF * c:HALF * c + HALF]
                    pe.wait_ge(relu_done, n + 1)
                    mm(zb[:, k, :], w1h[:, e, :], moving, start=True, stop=False)
                    mm(zb[:, k, :], w1l[:, e, :], moving, start=False, stop=True).then_inc(z_ps, 1)
                    pe.wait_ge(gated, n + 1)
                    mm(gb[:, k, :], sel[:, e, :], g3T[:, b, HALF * c:HALF * c + HALF],
                       start=True, stop=True).then_inc(g_ps, 1)

            def expert_out(b, s):
                c, p = s // NPAIR, s % NPAIR
                if p == 0:
                    pe.wait_ge(y_evac, 2 * b + c + 1)
                pe.wait_ge(gated, 32 * b + 2 * s + 4)
                for k in range(2):
                    last = mm(yb[D * k:D * k + D, :], w2s[:, 2 * p + k, :], hr[:, 2 * (s % 2) + k, :],
                              start=p == 0, stop=p == NPAIR - 1)
                last.then_inc(h_used, 1)
                if p == NPAIR - 1:
                    pass

            def moe_tokens(b, c):
                n = 2 * b + c
                pe.wait_ge(y_evac, n + 2)
                pe.wait_ge(moe_read, n + 1)
                for i in range(4):
                    o = A2[:, D * i:D * i + D]
                    mm(o, yT[:, P * i:P * i + P], dup2, start=True, stop=False)
                    for k in range(PARTS):
                        last = mm(o, g3T[:, b, HALF * c + P * i:HALF * c + P * i + P], b2p[:, k, :], start=False,
                                  stop=k == PARTS - 1)
                last.then_inc(moe_ps, 1)

            def stage_m(b, slot):
                if slot < STEPS - 1:
                    expert_in(b, slot + 1)
                expert_out(b, slot)
                if slot == NPAIR:
                    moe_tokens(b, 0)

            pe.wait_ge(l_cst, 16)
            pe.wait_ge(l_w18, 16)
            for i in range(8):
                if i >= 2:
                    pe.wait_ge(fold_sb, i - 1)
                mm((A0, A1)[i % 2][0:16, :], cst[0:18, C_DFT:C_DFT + 16], wt18[:, 8 * i:8 * i + 8, :],
                   start=True, stop=True).then_inc(fold_ps, 1)
            pe.wait_ge(lnc["out"], 1)
            pe.wait_ge(fold_sb, 8)
            pe.transpose(A2[:, 0:1], x1c[:, :, :], cst[0:1, C_ID:C_ID + 1]).then_inc(c_xT, 1)
            pe.wait_ge(c_xx, 1)
            pe.wait_ge(wmix_ok, 3)
            mm(A0[0:1, 0:P], XXc[:, :], wmix[:, 0:2, :], start=True, stop=True)
            for half in range(2):
                for j, i in enumerate((0, 2)):
                    last = mm(A1[D * half:D * half + D, j:j + 1], wmix[:, i, :], XXc[:, :], start=True, stop=True)
            last.then_inc(c_kv, 1)
            pe.wait_ge(c_kv0, 1)
            pe.wait_ge(G_ok, 1)
            for half in range(2):
                mm(A2[D * half:D * half + D, :], kv0t[:, 0, :], G[0:1, 1 + HALF * half:1 + HALF * half + HALF],
                   start=True, stop=True)
            mm(A1[0:D, 2:3], kv0t[:, 0, :], G[0:1, 0:1], start=True, stop=True).then_inc(c_C0, 1)
            pe.wait_ge(c_rw, 1)
            pe.wait_ge(l_wo, 32)
            mm(A0[0:1, 0:D], c0s[0:D, 3:4], wobd[0:D, 0:D], start=True, stop=True).then_inc(c_att, 1)
            pe.wait_ge(l_b, 64)
            pe.transpose(A1[:, 0:NE], b1row[:, :], cst[0:NE, C_ID:C_ID + NE]).then_inc(b1_ps, 1)
            pe.wait_ge(lnc["out"], 2)
            pe.wait_ge(c_C0sb, 1)
            pe.transpose(A2[:, 0:1], x2c[:, :, :], cst[0:1, C_ID:C_ID + 1]).then_inc(c_x2T, 1)
            pe.wait_ge(c_x2sb, 1)
            pe.wait_ge(l_gate, 80)
            mm(A2[0:1, 0:NE], x2cT[0:D, :], gw2[0:D, :], start=True, stop=True).then_inc(c_lg, 1)
            pe.wait_ge(b1_ok, 1)
            pe.wait_ge(l_w1, 32)
            for e in range(NE):
                last = mm(A1[:, e:e + 1], w1raw[0:D, e, :], x2cT[0:D, :], start=True, stop=True)
            last.then_inc(c_z, 1)
            pe.wait_ge(c_g, 4)
            mm(A2[:, 0:NE], ones[0:1, 0:P], gwc[:, 0, :], start=True, stop=True)
            pe.transpose(A2[0:NE, NE:NE + 1], gwc[:, 0, :], cst[0:1, C_ID:C_ID + 1]).then_inc(c_gT, 1)
            pe.wait_ge(c_gTsb, 1)
            pe.wait_ge(c_h, 1)
            pe.wait_ge(l_w2, 16)
            mm(A0[0:1, 0:D], gTc[:, :], b2x3[0:NE, :], start=True, stop=False)
            for e in range(NE):
                last = mm(A0[0:1, 0:D], hc[:, e:e + 1], w2s[:, e, :], start=False, stop=e == NE - 1)
            last.then_inc(c_moe, 1)
            pe.wait_ge(c_y, 1)
            pe.wait_ge(l_wf, 256)
            for g in range(16):
                stage_a(0, g)
            pe.wait_ge(w1l_ok, 1)
            pe.wait_ge(b2_ok, 4)

            def batch(b, with_next):
                pe.wait_ge(xs_kept, b + 1)
                pe.wait_ge(g3T_done, b + 1)
                expert_in(b, 0)
                for slot in range(STEPS):
                    stage_m(b, slot)
                    if with_next:
                        stage_a(b + 1, slot)
                moe_tokens(b, 1)

            with pe.Fori(0, NB - 1) as b:
                batch(b, True)
            batch(NB - 1, False)

        @block.scalar
        def _(act):
            fn = act.activation

            def stage_a(b, g):
                if g == 0:
                    act.wait_ge(uv_ps, 3 * b + 1)
                    fn(uv_v[0:D, 0:8, :], A0[0:D, :].rearrange("p (m v) -> p m v", m=8), ACT.Copy).then_inc(u_done, 1)
                elif g == 1:
                    act.wait_ge(uv_ps, 3 * b + 2)
                    fn(uv_v[0:D, 8:16, :], A1[0:D, :].rearrange("p (m v) -> p m v", m=8), ACT.Copy).then_inc(u_done, 1)
                elif g == 2:
                    act.wait_ge(h_ps, b + 1)
                    fn(h[:, :, :], A1[:, :].rearrange("p (i d) -> p i d", d=D), ACT.Copy).then_inc(h_done, 1)
                elif g == 3:
                    ln_square(act, ln1, b, xc[:, :, :], sq[:, :, :])
                elif g == 4:
                    for c in range(2):
                        act.wait_ge(x1_ps, 2 * b + c + 1)
                        fn(XX[0:D, HALF * c:HALF * c + HALF], (A0, A1)[c][0:D, :], ACT.Copy).then_inc(xx_lo, 1)
                elif g == 5:
                    for c in range(2):
                        act.wait_ge(kt_clip, 2 * b + c + 1)
                        fn(kt[:, 4 * c:4 * c + 4, :], kt[:, 4 * c:4 * c + 4, :], ACT.Exp).then_inc(kt_exp, 1)
                elif g == 6:
                    act.wait_ge(kc_clip, b + 1)
                    fn(kc[:, :], kc[:, :], ACT.Exp).then_inc(kc_exp, 1)
                    act.wait_ge(r_ps, b + 1)
                    fn(er[:, :], A1[:, :], ACT.Exp, scale=-1.0).then_inc(er_done, 1)
                elif g == 11:
                    ln_square(act, ln2, b, xc[:, :, :], sq[:, :, :])
                elif g == 12:
                    if not isinstance(b, int):
                        act.wait_ge(xs_kept, b)
                    for c in range(2):
                        act.wait_ge(x2_ps, 2 * b + c + 1)
                        fn(xstk[:, HALF * c:HALF * c + HALF], (A1, A0)[c][:, :], ACT.Copy).then_inc(xs_hi, 1)
                elif g == 14:
                    act.wait_ge(gap_done, b + 1)
                    fn(gsm[:, 1, :], gsm[:, 0, :], ACT.Exp).then_inc(gexp, 1)
                elif g == 15:
                    act.wait_ge(g3_ps, b + 1)
                    fn(g3T[:, b, :], A0b[:, :], ACT.Copy).then_inc(g3T_done, 1)

            def relu(b, s):
                p = s % NPAIR
                act.wait_ge(h_used, 16 * b + s + 1)
                for k in range(2):
                    act.wait_ge(z_ps, 32 * b + 2 * s + k + 1)
                    fn(hr[:, 2 * (s % 2) + k, :], zb[:, k, :], ACT.Relu,
                       bias=b1T[:, 2 * p + k:2 * p + k + 1]).then_inc(relu_done, 1)

            def y_out(b, c):
                act.wait_ge(h_used, 16 * b + NPAIR * (c + 1) + 2)
                act.wait_ge(moe_ps, 2 * b + c + 1)
                fn(yT[:, :], yb[:, :], ACT.Copy).then_inc(y_evac, 1)

            def stage_m(b, slot):
                if slot < STEPS - 1:
                    relu(b, slot + 1)
                if slot % NPAIR == NPAIR - 1:
                    y_out(b, slot // NPAIR)
                if slot == NPAIR + 2:
                    ln_square(act, ln3, 2 * b, y3c[:, :, :], y3q[:, :, :])

            act.wait_ge(l_cls, 16)
            ln_square(act, lnc, 0, clw[:, 0:1, :], clw[:, 1:2, :])
            for i in range(8):
                act.wait_ge(fold_ps, i + 1)
                fn(wfp[:, :, 8 * i:8 * i + 8].rearrange("p c o -> p o c"),
                   (A0, A1)[i % 2][0:16, :].rearrange("p (o c) -> p o c", c=D), ACT.Copy).then_inc(fold_sb, 1)
            act.wait_ge(c_xT, 1)
            fn(XX[D:P, 0:1], A2[D:P, 0:1], ACT.Copy)
            act.wait_ge(zeroed, 6)
            fn(XXc[0:D, :], A2[0:D, 0:1], ACT.Copy).then_inc(c_xx, 1)
            act.wait_ge(c_clip, 2)
            fn(kv0t[:, 1, :], kv0t[:, 1, :], ACT.Exp)
            fn(k0[:, :], k0[:, :], ACT.Exp)
            fn(c0s[:, 0:1], A1[:, 1:2], ACT.Exp, scale=-1.0).then_inc(c_exp, 1)
            act.wait_ge(c_C0, 1)
            fn(C0[:, :], A2[:, :], ACT.Copy).then_inc(c_C0sb, 1)
            act.wait_ge(b1_ps, 1)
            fn(b1T[:, :], A1[:, 0:NE], ACT.Copy).then_inc(b1_ok, 1)
            ln_square(act, lnc, 1, clw[:, 0:1, :], clw[:, 1:2, :])
            act.wait_ge(c_x2T, 1)
            fn(x2cT[:, :], A2[:, 0:1], ACT.Copy).then_inc(c_x2sb, 1)
            act.wait_ge(c_gate, 4)
            fn(gsmc[:, 1, :], gsmc[:, 0, :], ACT.Exp).then_inc(c_gexp, 1)
            act.wait_ge(c_gT, 1)
            fn(gTc[:, :], A2[0:NE, NE:NE + 1], ACT.Copy)
            fn(gbc[:, :], A2[:, 0:NE], ACT.Copy).then_inc(c_gTsb, 1)
            act.wait_ge(l_w1, 32)
            fn(w1h[:, :, :], w1raw[:, :, :], ACT.Copy).then_inc(w1h_ok, 1)
            ln_square(act, lnc, 2, y3cl[:, 1:2, :], y3cl[:, 2:3, :])
            for g in range(16):
                stage_a(0, g)

            def batch(b, with_next):
                relu(b, 0)
                for slot in range(STEPS):
                    stage_m(b, slot)
                    if with_next:
                        stage_a(b + 1, slot)
                ln_square(act, ln3, 2 * b + 1, y3c[:, :, :], y3q[:, :, :])

            with act.Fori(0, NB - 1) as b:
                batch(b, True)
            batch(NB - 1, False)

        @block.vector
        def _(dve):
            tt, ts, stt = dve.tensor_tensor, dve.tensor_scalar, dve.scalar_tensor_tensor

            def gate_top(lgt, top, idx, n_tiles, n0, s_top, s_idx):
                for i in range(n_tiles):
                    dve.max(top[:, i, :], lgt[:, i, :]).then_inc(s_top, 1)
                for i in range(n_tiles):
                    settle(dve, s_top, n0 + i + 1)
                    dve.max_index(idx[:, i, :], top[:, i, :], lgt[:, i, :]).then_inc(s_idx, 1)

            def stage_a(b, g):
                if g == 0:
                    dve.wait_ge(uv_ps, 3 * b + 1)
                    dve.tensor_copy(uv_v[D:P, 0:7, :],
                                    A0[D:P, :].rearrange("p (m v) -> p m v", m=8)[:, 1:8, :]).then_inc(v_done, 1)
                elif g == 1:
                    dve.wait_ge(uv_ps, 3 * b + 2)
                    dve.tensor_copy(uv_v[D:P, 7:15, :],
                                    A1[D:P, :].rearrange("p (m v) -> p m v", m=8)).then_inc(v_done, 1)
                    dve.wait_ge(uv_ps, 3 * b + 3)
                    dve.tensor_copy(uv_v[D:P, 15, :], A0[D:P, 0:VARS]).then_inc(v_done, 1)
                elif g == 2:
                    dve.wait_ge(h_done, b + 1)
                    ln_center(dve, ln1, b, h[:, :, :], stat, xc[:, :, :], P, NT)
                elif g == 3:
                    ln_var(dve, ln1, b, sq[:, :, :], stat, P)
                    ln_scale(dve, ln1, b, xc[:, :, :], stat, [x1[:, :, 0, :], x1[:, :, 1, :]], P, NT)
                elif g == 4:
                    for c in range(2):
                        dve.wait_ge(x1_ps, 2 * b + c + 1)
                        n = HALF - c
                        dve.tensor_copy(XX[D:P, 1 + HALF * c:1 + HALF * c + HALF],
                                        (A0, A1)[c][D:P, :]).then_inc(xx_hi, 1)
                elif g == 5:
                    for c in range(2):
                        bank = (A0, A1)[c][:, :].rearrange("p (i w d) -> p i w d", i=4, w=2)
                        ks = kt[:, 4 * c:4 * c + 4, :]
                        dve.wait_ge(kv_ps, 2 * b + c + 1)
                        ts(ks, bank[:, :, 0, :], -60.0, 30.0, ALU.max, ALU.min).then_inc(kt_clip, 1)
                    for c in range(2):
                        bank = (A0, A1)[c][:, :].rearrange("p (i w d) -> p i w d", i=4, w=2)
                        dve.wait_ge(kt_exp, 2 * b + c + 1)
                        tt(kv[:, 4 * c:4 * c + 4, :], kt[:, 4 * c:4 * c + 4, :], bank[:, :, 1, :],
                           ALU.mult).then_inc(kv_done, 1)
                elif g == 6:
                    dve.wait_ge(kc_ps, b + 1)
                    ts(kc[:, :], A0[:, :], -60.0, 30.0, ALU.max, ALU.min).then_inc(kc_clip, 1)
                elif g == 7:
                    dve.wait_ge(carry_ps, b + 1)
                    tt(kinit[D:P, :], A0[D:P, 0:1], k0[D:P, :], ALU.add).then_inc(kinit_ok, 1)
                    dve.wait_ge(kinit_ok, b + 1)
                    dve.wait_ge(kc_exp, b + 1)
                    dve.tensor_tensor_scan(sk[:, :], ones[:, :], kc[:, :], kinit[:, :], ALU.mult,
                                           ALU.add).then_inc(sk_done, 1)
                    dve.wait_ge(sk_done, b + 1)
                    dve.wait_ge(er_done, b + 1)
                    stt(er[:, :], er[:, :], 1.0, sk[:, :], ALU.add, ALU.mult).then_inc(q_done, 1)
                elif g == 8:
                    dve.wait_ge(q_done, b + 1)
                    dve.reciprocal(rq[:, :], er[:, :]).then_inc(rq_done, 1)
                elif g == 9:
                    dve.wait_ge(wkv_ps, b + 1)
                    tt(wsum[:, :], A1[:, :], C0[:, :], ALU.add).then_inc(wsum_done, 1)
                    dve.wait_ge(wsum_done, b + 1)
                    dve.wait_ge(rq_done, b + 1)
                    tt(rw[:, :], wsum[:, :], rq[:, :], ALU.mult).then_inc(rw_done, 1)
                elif g == 10:
                    dve.wait_ge(att_ps, b + 1)
                    for half in range(2):
                        last = tt(h1[:, b, 4 * half:4 * half + 4, :],
                                  A0[:, :].rearrange("p (i s d) -> p s i d", i=4, s=2)[:, half, :, :],
                                  h[:, 4 * half:4 * half + 4, :], ALU.add)
                    last.then_inc(h1_done, 1)
                    settle(dve, h1_done, b + 1)
                    ln_center(dve, ln2, b, h1[:, b, :, :], stat, xc[:, :, :], P, NT)
                elif g == 11:
                    ln_var(dve, ln2, b, sq[:, :, :], stat, P)
                    if not isinstance(b, int):
                        dve.wait_ge(x2_kept, b)
                    ln_scale(dve, ln2, b, xc[:, :, :], stat, [x2s[:, :, 0, :], x2s[:, :, 1, :]], P, NT)
                elif g == 12:
                    for c in range(2):
                        lo = xstk[D:P, HALF * c:HALF * c + HALF]
                        dve.wait_ge(xs_hi, 2 * b + c + 1)
                        tt(lo, (A1, A0)[c][D:P, :], lo.bitcast(F32), ALU.subtract).then_inc(xs_lo, 1)
                elif g == 13:
                    dve.wait_ge(lg_ps, b + 1)
                    tt(lg[:, :, :], A1[:, 0:P].rearrange("p (i e) -> p i e", e=NE),
                       gbb[:, :].unsqueeze(1).broadcast_to([P, NT, NE]), ALU.add).then_inc(lg_done, 1)
                    settle(dve, lg_done, b + 1)
                    gate_top(lg, top8, idx8, NT, NT * b, top_done, idx_done)
                    tt(gsm[:, 0, :], top8[:, :, 1], top8[:, :, 0], ALU.subtract).then_inc(gap_done, 1)
                    dve.wait_ge(idx_done, NT * b + NT)
                    dve.tensor_copy(idxf[:, :, :], idx8[:, :, 0:2]).then_inc(idxf_done, 1)
                elif g == 14:
                    dve.wait_ge(idxf_done, b + 1)
                    for k, row in enumerate((eq1, eq2)):
                        tt(row[:, :, :], iota[:, :].unsqueeze(1).broadcast_to([P, NT, NE]),
                           idxf[:, :, k:k + 1].broadcast_to([P, NT, NE]), ALU.is_equal).then_inc(eq_done, 1)
                    dve.wait_ge(gexp, b + 1)
                    ts(gsm[:, 2, :], gsm[:, 1, :], 1.0, None, ALU.add).then_inc(gden, 1)
                    dve.wait_ge(gden, b + 1)
                    dve.reciprocal(gsm[:, 3, :], gsm[:, 2, :]).then_inc(g1_done, 1)
                    dve.wait_ge(g1_done, b + 1)
                    tt(gsm[:, 2, :], gsm[:, 1, :], gsm[:, 3, :], ALU.mult).then_inc(g2_done, 1)
                    dve.wait_ge(eq_done, 2 * b + 2)
                    dve.wait_ge(g2_done, b + 1)
                    for row, w in ((eq1, gsm[:, 3, :]), (eq2, gsm[:, 2, :])):
                        last = tt(row[:, :, :], row[:, :, :], w.unsqueeze(2).broadcast_to([P, NT, NE]), ALU.mult)
                    last.then_inc(eqg_done, 1)
                    dve.wait_ge(eqg_done, b + 1)
                    tt(gw[:, :, :], eq1[:, :, :], eq2[:, :, :], ALU.add).then_inc(gw_done, 1)
                    dve.wait_ge(gw_done, b + 1)
                    dve.tensor_copy(g3[:, :, 0:NE], gw[:, :, :]).then_inc(gh_done, 1)
                    dve.wait_ge(gh_done, b + 1)
                    tt(grem[:, :, :], gw[:, :, :], g3[:, :, 0:NE], ALU.subtract).then_inc(gr_done, 1)
                    dve.wait_ge(gr_done, b + 1)
                    dve.tensor_copy(g3[:, :, NE:2 * NE], grem[:, :, :]).then_inc(gm_done, 1)
                    dve.wait_ge(gm_done, b + 1)
                    tt(g3[:, :, 2 * NE:3 * NE], grem[:, :, :], g3[:, :, NE:2 * NE], ALU.subtract).then_inc(g3_done, 1)

            def gate(b, s):
                for k in range(2):
                    n = 32 * b + 2 * s + k
                    t = hr[:, 2 * (s % 2) + k, :]
                    dve.wait_ge(relu_done, n + 3)
                    dve.wait_ge(g_ps, n + 1)
                    tt(t, t, gb[:, k, :], ALU.mult).then_inc(gated, 1)

            def ln3_begin(b, c):
                n = 2 * b + c
                dve.wait_ge(moe_ps, n + 2)
                tt(y3[:, :, :], A2[:, 0:4 * D].rearrange("p (i d) -> p i d", d=D), x2[:, b, 4 * c:4 * c + 4, :],
                   ALU.add).then_inc(moe_read, 1)
                dve.wait_ge(moe_read, n + 2)
                ln_center(dve, ln3, n, y3[:, :, :], stat3, y3c[:, :, :], P, 4)

            def ln3_end(b, c):
                n = 2 * b + c
                dve.wait_ge(yg_done, n + 1)
                ln_scale(dve, ln3, n, y3c[:, :, :], stat3, [yn[:, :, :]], P, 4)

            def stage_m(b, slot):
                if slot < STEPS - 1:
                    gate(b, slot + 1)
                if slot == NPAIR + 1:
                    ln3_begin(b, 0)
                if slot == NPAIR + 2:
                    ln_var(dve, ln3, 2 * b, y3q[:, :, :], stat3, P)
                if slot == NPAIR + 3:
                    ln3_end(b, 0)

            dve.memset(ones[:, :], 1.0).then_inc(ones_ok, 1)
            dve.wait_ge(l_cst, 16)
            dve.tensor_copy(identb[:, :], ident)
            dve.tensor_copy(sel[:, :, :], cst[:, C_I3:C_I3 + NE].unsqueeze(2).broadcast_to([P, NE, P])).then_inc(cst_ready, 1)
            dve.wait_ge(l_cls, 16)
            ln_center(dve, lnc, 0, cl[:, :].unsqueeze(1), cls4, clw[:, 0:1, :], 1, 1)
            dve.wait_ge(l_tw, 16)
            n0 = KPAD + 1 - WLEN
            dve.tensor_copy(padrow[:, 0:n0], twrow[:, 0:1].broadcast_to([1, n0])).then_inc(pad_ok, 1)
            dve.tensor_copy(padrow[:, n0:n0 + WLEN], twrow[:, :]).then_inc(pad_ok, 1)
            dve.memset(padrow[:, n0 + WLEN:], 0.0).then_inc(pad_ok, 1)
            ln_var(dve, lnc, 0, clw[:, 1:2, :], cls4, 1)
            ln_scale(dve, lnc, 0, clw[:, 0:1, :], cls4, [x1c[:, 0:1, :], x1c[:, 1:2, :]], 1, 1)
            dve.wait_ge(l_mix, 16 * 12)
            ts(mixf[D:P, :], mixf[D:P, :], -1.0, 1.0, ALU.mult, ALU.add).then_inc(mixf_ok, 1)
            dve.wait_ge(mixf_ok, 1)
            for i in range(3):
                ts(wmix[:, i, :], wraw[:, i, :], mixf[:, i:i + 1], None, ALU.mult).then_inc(wmix_ok, 1)
            dve.wait_ge(l_grev, 16)
            dve.tensor_copy(G[:, :], grev[:, ::-1]).then_inc(G_ok, 1)
            dve.wait_ge(c_kv, 1)
            ts(kv0t[:, 1, :], A0[0:1, 0:D], -60.0, 30.0, ALU.max, ALU.min).then_inc(c_clip, 1)
            ts(k0[:, :], A1[:, 0:1], -60.0, 30.0, ALU.max, ALU.min).then_inc(c_clip, 1)
            dve.wait_ge(c_exp, 1)
            tt(kv0t[:, 0, :], kv0t[:, 1, :], A0[0:1, D:P], ALU.mult).then_inc(c_kv0, 1)
            dve.tensor_copy(kinit[0:D, :], k0[0:D, :])
            stt(c0s[:, 1:2], c0s[:, 0:1], 1.0, k0[:, :], ALU.add, ALU.mult).then_inc(c_q, 1)
            dve.wait_ge(c_q, 1)
            dve.reciprocal(c0s[:, 2:3], c0s[:, 1:2]).then_inc(c_q, 1)
            dve.wait_ge(c_q, 2)
            dve.wait_ge(c_C0, 1)
            tt(c0s[0:D, 3:4], A1[0:D, 2:3], c0s[0:D, 2:3], ALU.mult).then_inc(c_rw, 1)
            dve.wait_ge(c_att, 1)
            tt(h1c[:, :], A0[0:1, 0:D], cl[:, :], ALU.add).then_inc(c_h1, 1)
            dve.wait_ge(c_h1, 1)
            ln_center(dve, lnc, 1, h1c[:, :].unsqueeze(1), cls4, clw[:, 0:1, :], 1, 1)
            ln_var(dve, lnc, 1, clw[:, 1:2, :], cls4, 1)
            ln_scale(dve, lnc, 1, clw[:, 0:1, :], cls4, [x2c[:, 0:1, :], x2c[:, 1:2, :]], 1, 1)
            dve.wait_ge(c_lg, 1)
            tt(lgc[:, 0, :], A2[0:1, 0:NE], gbb[0:1, :], ALU.add).then_inc(c_gate, 1)
            dve.wait_ge(c_gate, 1)
            gate_top(lgc, top8c, idx8c, 1, 1, c_gate, c_gate)
            tt(gsmc[:, 0, :], top8c[:, :, 1], top8c[:, :, 0], ALU.subtract).then_inc(c_gate, 1)
            dve.wait_ge(c_gate, 4)
            dve.tensor_copy(idxfc[:, :, :], idx8c[:, :, 0:2]).then_inc(c_gate, 1)
            dve.wait_ge(c_gate, 5)
            dve.wait_ge(zeroed, 6)
            for k in range(2):
                ts(eqc[:, k, :], iota[0:1, :], idxfc[:, 0, k:k + 1], None, ALU.is_equal)
            dve.wait_ge(c_gexp, 1)
            ts(gsmc[:, 2, :], gsmc[:, 1, :], 1.0, None, ALU.add).then_inc(c_g, 1)
            dve.wait_ge(c_g, 1)
            dve.reciprocal(gsmc[:, 3, :], gsmc[:, 2, :]).then_inc(c_g, 1)
            dve.wait_ge(c_g, 2)
            tt(gsmc[:, 2, :], gsmc[:, 1, :], gsmc[:, 3, :], ALU.mult)
            ts(gwc[:, 0, :], eqc[:, 0, :], gsmc[:, 3, :], None, ALU.mult).then_inc(c_g, 1)
            dve.wait_ge(c_g, 3)
            stt(gwc[:, 0, :], eqc[:, 1, :], gsmc[:, 2, :], gwc[:, 0, :], ALU.mult, ALU.add).then_inc(c_g, 1)
            dve.wait_ge(c_z, 1)
            dve.wait_ge(b1_ok, 1)
            tt(zc[:, :], A1[:, 0:NE], b1T[:, :], ALU.add).then_inc(c_zb, 1)
            dve.wait_ge(c_zb, 1)
            dve.wait_ge(c_gTsb, 1)
            stt(hc[:, :], zc[:, :], 0.0, gbc[:, :], ALU.max, ALU.mult).then_inc(c_h, 1)
            dve.wait_ge(w1h_ok, 1)
            tt(w1l[:, :, :], w1raw[:, :, :], w1h[:, :, :].bitcast(F32), ALU.subtract).then_inc(w1l_ok, 1)
            dve.tensor_copy(b2p[:, 0, :], b2x3[:, :]).then_inc(b2_ok, 1)
            dve.wait_ge(b2_ok, 1)
            tt(b2rem[:, :], b2x3[:, :], b2p[:, 0, :], ALU.subtract).then_inc(b2_ok, 1)
            dve.wait_ge(b2_ok, 2)
            dve.tensor_copy(b2p[:, 1, :], b2rem[:, :]).then_inc(b2_ok, 1)
            dve.wait_ge(b2_ok, 3)
            tt(b2p[:, 2, :], b2rem[:, :], b2p[:, 1, :], ALU.subtract).then_inc(b2_ok, 1)
            dve.wait_ge(c_moe, 1)
            tt(y3cl[:, 0, :], A0[0:1, 0:D], x2c[:, 0, :], ALU.add).then_inc(c_y, 1)
            dve.wait_ge(c_y, 1)
            ln_center(dve, lnc, 2, y3cl[:, 0:1, :], cls4, y3cl[:, 1:2, :], 1, 1)
            ln_var(dve, lnc, 2, y3cl[:, 2:3, :], cls4, 1)
            ln_scale(dve, lnc, 2, y3cl[:, 1:2, :], cls4, [y3cl[:, 0:1, :]], 1, 1)
            dve.wait_ge(lnc["out"], 3)
            tt(y3cl[:, 1, :], y3cl[:, 0, :], gam[0:1, :], ALU.mult).then_inc(c_fin, 1)
            dve.wait_ge(c_fin, 1)
            tt(y3cl[:, 2, :], y3cl[:, 1, :], bet[0:1, :], ALU.add).then_inc(c_fin, 1)
            dve.wait_ge(c_fin, 2)
            tt(y3cl[:, 3, :], y3cl[:, 2, :], h1c[:, :], ALU.add).then_inc(c_fo, 1)
            for g in range(16):
                stage_a(0, g)

            def batch(b, with_next):
                gate(b, 0)
                for slot in range(STEPS):
                    stage_m(b, slot)
                    if with_next:
                        stage_a(b + 1, slot)
                ln3_begin(b, 1)
                ln_var(dve, ln3, 2 * b + 1, y3q[:, :, :], stat3, P)
                ln3_end(b, 1)

            with dve.Fori(0, NB - 1) as b:
                batch(b, True)
            batch(NB - 1, False)

        @block.gpsimd
        def _(pool):
            def stage_a(b, g):
                if g == 3:
                    ln_rstd(pool, ln1, b, stat, P, NT)
                elif g == 11:
                    ln_rstd(pool, ln2, b, stat, P, NT)
                    pool.wait_ge(ln2["out"], b + 1)
                    pool.tensor_copy(x2[:, b, :, :], x2s[:, :, 0, :]).then_inc(x2_kept, 1)
                elif g == 12:
                    pool.wait_ge(xs_lo, 2 * b + 2)
                    pool.tensor_copy(xs[:, b, :], xstk[:, :].bitcast(F32)).then_inc(xs_kept, 1)
                elif g == 15:
                    pool.tensor_tensor(h1[:, b, :, :], h1[:, b, :, :],
                                       bet[:, :].unsqueeze(1).broadcast_to([P, NT, D]), ALU.add).then_inc(h1b_done, 1)

            def finish(b, c):
                n = 2 * b + c
                ln_rstd(pool, ln3, n, stat3, P, 4)
                pool.wait_ge(ln3["out"], n + 1)
                pool.tensor_tensor(yg[:, :, :], yn[:, :, :], gam[:, :].unsqueeze(1).broadcast_to([P, 4, D]),
                                   ALU.mult).then_inc(yg_done, 1)
                pool.wait_ge(yg_done, n + 2)
                pool.wait_ge(stored, 16 * n + 16)
                pool.tensor_tensor(fo[:, :, :], yg[:, :, :], h1[:, b, 4 * c:4 * c + 4, :],
                                   ALU.add).then_inc(fo_done, 1)

            def stage_m(b, slot):
                if slot == NPAIR + 3:
                    finish(b, 0)

            for i, (counter, free) in enumerate(((relu_done, 2), (gated, 2), (h_used, 2), (y_evac, 1), (moe_ps, 1), (moe_read, 1),
                                  (yg_done, 1), (stored, 16))):
                pool.memset(spare[:, i:i + 1], 0.0).then_inc(counter, free)
            pool.memset(mhalf[:, :], -0.5).then_inc(zeroed, 1)
            for tile in (XXc, wobd, b2x3):
                pool.memset(tile[:, :], 0.0).then_inc(zeroed, 1)
            pool.memset(g3[:, :, :], 0.0).then_inc(zeroed, 1)
            pool.iota(iota[:, :], [[1, NE]], base=0, channel_multiplier=0,
                      allow_small_or_imprecise_dtypes=True).then_inc(zeroed, 1)
            pool.wait_ge(zeroed, 6)
            for n in range(3):
                ln_rstd(pool, lnc, n, cls4, 1, 1)
            for g in range(16):
                stage_a(0, g)
            pool.wait_ge(l_gate, 80)

            def batch(b, with_next):
                for slot in range(STEPS):
                    stage_m(b, slot)
                    if with_next:
                        stage_a(b + 1, slot)
                finish(b, 1)

            with pool.Fori(0, NB - 1) as b:
                batch(b, True)
            batch(NB - 1, False)


_INS = ["x", "cls_tok", "L0_tok_W", "L0_attn_time_w", "L0_attn_time_mix_k", "L0_attn_time_mix_v",
        "L0_attn_time_mix_r", "L0_attn_Wk", "L0_attn_Wv", "L0_attn_Wr", "L0_attn_Wo", "L0_ffn_gate_w",
        "L0_ffn_gate_b", "L0_ffn_w1", "L0_ffn_b1", "L0_ffn_w2", "L0_ffn_b2", "L0_ffn_gamma", "L0_ffn_beta"]


def _constants(np):
    c = np.zeros((P, C_END), np.float32)
    c[:, C_ID:C_ID + P] = np.eye(P)
    c[:, C_DUP:C_DUP + D] = np.tile(np.eye(D), (2, 1))
    c[0:PARTS * NE, C_I3:C_I3 + NE] = np.tile(np.eye(NE), (PARTS, 1))
    angle = 2 * np.pi * np.arange(9)[:, None] * np.arange(16)[None, :] / 16
    c[0:9, C_DFT:C_DFT + 16] = np.cos(angle) / 4
    c[9:18, C_DFT:C_DFT + 16] = -np.sin(angle) / 4
    return c


def kernel(**inputs):
    import numpy as _np
    import concourse.bacc as _bacc
    from concourse.bass_utils import run_bass_kernel_spmd as _run

    nc = _bacc.Bacc("TRN2", target_bir_lowering=False, num_devices=1)
    arrays, args = {}, []
    for name in _INS:
        a = _np.ascontiguousarray(inputs[name])
        arrays[f"in_{name}"] = a
        args.append(nc.dram_tensor(f"in_{name}", a.shape, mybir.dt.from_np(a.dtype), kind="ExternalInput").ap())
    arrays["in_consts"] = _constants(_np)
    args.append(nc.dram_tensor("in_consts", (P, C_END), F32, kind="ExternalInput").ap())
    args.append(nc.dram_tensor("padded_time_w", (1, KPAD + P), F32, kind="Internal").ap())
    args.append(nc.dram_tensor("out_tokens", (NB, TOK + 1, D), F32, kind="ExternalOutput").ap())
    build(nc, *args)
    r = _run(nc, [arrays], core_ids=[0])
    return r.results[0]["out_tokens"]
```

```python
from contextlib import ExitStack

import concourse.bass as bass
from concourse import mybir

F32 = mybir.dt.float32
F32R = mybir.dt.float32r
U32 = mybir.dt.uint32
ALU = mybir.AluOpType
ACT = mybir.ActivationFunctionType
AX_X = mybir.AxisListType.X

P = 128
D = 64
NB = 4
VARS = 64
UV = VARS // 2
NPATCH = 16
TOK = VARS * NPATCH
UT = TOK // 2
NT = UT // P
Q = UT // 2
NU = 2 * NB
NE = 16
NPAIR = NE // 2
FF = 128
WLEN = 512
KPAD = 1024
EPS = 1e-5
C_ID, C_DUP, C_DFT, C_TOKW, C_END = 0, 128, 192, 256, 1280
S_W, S_MIX, S_WO, S_GW, S_GB, S_GAM, S_BET, S_B1, S_B2, S_CLS, S_END = (
    0, 192, 195, 323, 339, 355, 419, 483, 499, 563, 627)

WINDOW = (
    ("A2", "wkv"),
    ("M", "in", 1), ("M", "out", 0), ("A1", "embed"),
    ("M", "in", 2), ("M", "out", 1), ("A2", "att"), ("A1", "edge"),
    ("M", "in", 3), ("A2", "var"), ("M", "out", 2),
    ("M", "in", 4), ("A1", "tokens"), ("A2", "scale"), ("A1", "var"), ("M", "out", 3),
    ("M", "in", 5), ("M", "out", 4), ("A2", "turn"),
    ("M", "in", 6), ("A1", "scale"), ("M", "out", 5), ("A2", "logits"),
    ("M", "in", 7), ("A1", "turn"), ("M", "out", 6), ("A2", "gates"), ("M", "out", 7),
    ("M", "in", 8), ("A1", "kv"), ("A2", "spread"), ("A1", "kr"), ("A1", "carry"), ("M", "tokens"), ("M", "center"),
    ("M", "var"), ("A1", "rq"), ("M", "scale"),
)
FILL = (
    ("C", 0, "mix"), ("C", 0, "norm"), ("A1", 0, "embed"), ("C", 0, "edge"), ("A1", 0, "edge"), ("C", 0, "turn"),
    ("A1", 0, "tokens"), ("A1", 0, "var"), ("C", 0, "z0"), ("C", 0, "w1"), ("A1", 0, "scale"), ("A1", 0, "turn"),
    ("C", 0, "gates"), ("A1", 0, "kv"), ("A1", 0, "kr"), ("A1", 0, "carry"), ("A1", 0, "rq"), ("A2", 0, "wkv"),
    ("C", 0, "z1"), ("A2", 0, "att"), ("A1", 1, "embed"), ("A2", 0, "var"), ("A2", 0, "scale"), ("A2", 0, "turn"),
    ("C", 0, "spread"), ("A1", 1, "edge"), ("A2", 0, "logits"), ("A1", 1, "tokens"), ("A2", 0, "gates"),
    ("A1", 1, "var"), ("A2", 0, "spread"), ("A1", 1, "scale"), ("C", 0, "y0"), ("A1", 1, "turn"), ("C", 0, "y1"),
    ("A1", 1, "kv"), ("C", 0, "out"), ("C", 0, "experts"), ("A1", 1, "kr"), ("A1", 1, "carry"), ("A1", 1, "rq"),
)


def build(nc, x, time_row, w1, w2, consts, small, folded, spread, out):
    with ExitStack() as ctx:
        def sb(name, shape, dt=F32):
            return ctx.enter_context(nc.sbuf_tensor(name, shape, dt))

        def psum(name, shape, dt=F32):
            return ctx.enter_context(nc.psum_tensor(name, shape, dt))

        def sem(name):
            return ctx.enter_context(nc.semaphore(name))

        cst = sb("cst", [P, C_END])
        ident = cst[:, C_ID:C_ID + P]
        dup2 = cst[:, C_DUP:C_DUP + D]
        par = sb("par", [P, S_END])
        wobd = par[:, S_WO:S_WO + P]
        gw2 = par[:, S_GW:S_GW + NE]
        gbb = par[:, S_GB:S_GB + NE]
        gam = par[:, S_GAM:S_GAM + D]
        bet = par[:, S_BET:S_BET + D]
        b1T = par[:, S_B1:S_B1 + NE]
        b2s = par[0:NE, S_B2:S_B2 + D]
        cl = par[0:1, S_CLS:S_CLS + D]
        iota = sb("iota", [P, NE])
        ones = sb("ones", [P, Q])
        spare = sb("spare", [P, 12])
        mhalf = sb("mhalf", [P, NT])
        wfp = sb("wfp", [D, 2 * UT])
        wf = sb("wf", [P, 4, 2, D])
        wfe = sb("wfe", [P, 3, P])
        wmix = sb("wmix", [P, 3, D])
        grev = sb("grev", [P, KPAD + 1])
        G = sb("G", [P, KPAD + 1])
        w1raw = sb("w1raw", [P, NE, FF])
        w1h = sb("w1h", [P, NE, FF], F32R)
        w1l = sb("w1l", [P, NE, FF], F32R)
        w2s = sb("w2s", [P, NE, D])

        xt = sb("xt", [P, 16, 4 * VARS])
        uv = sb("uv", [P, UT])
        h = sb("h", [P, 2, NT, D])
        xc1, xc2 = sb("xc1", [P, NT, D]), sb("xc2", [P, NT, D])
        sq1, sq2 = sb("sq1", [P, NT, D]), sb("sq2", [P, NT, D])
        st1, st2 = sb("st1", [P, 4, NT]), sb("st2", [P, 4, NT])
        x1 = sb("x1", [P, NT, 2, D])
        XX = sb("XX", [P, TOK + 1])
        kt = sb("kt", [P, NT, D])
        kv = sb("kv", [P, 2, NT, D])
        kc = sb("kc", [P, Q])
        sk = sb("sk", [P, 2, Q])
        kinit = sb("kinit", [P, 2])
        er = sb("er", [P, Q])
        rq = sb("rq", [P, Q])
        C0 = sb("C0", [P, 2, Q])
        wsum = sb("wsum", [P, Q])
        rw = sb("rw", [P, Q])
        h1 = sb("h1", [P, NT, D])
        h1b = sb("h1b", [P, 2, NT, D])
        x2s = sb("x2s", [P, 2, NT, 2, D])
        xs = sb("xs", [P, 2, UT], F32R)
        lg = sb("lg", [P, NT, NE])
        top8 = sb("top8", [P, NT, 8])
        idx8 = sb("idx8", [P, NT, 8], U32)
        idxf = sb("idxf", [P, NT, 2])
        gsm = sb("gsm", [P, 4, NT])
        eq1 = sb("eq1", [P, NT, NE])
        eq2 = sb("eq2", [P, NT, NE])
        gw = sb("gw", [P, NT, NE])
        gT = sb("gT", [NE, 2, UT])
        gbs = sb("gbs", [P, 2, NPAIR, UT])

        hr = sb("hr", [P, 4, UT])
        prod = sb("prod", [P, 2, UT])
        acc = sb("acc", [P, 2, UT])
        y3 = sb("y3", [P, NT, D])
        y3c = sb("y3c", [P, NT, D])
        y3q = sb("y3q", [P, NT, D])
        st3 = sb("st3", [P, 4, NT])
        yn = sb("yn", [P, NT, D])
        yg = sb("yg", [P, NT, D])
        fo = sb("fo", [P, NT, D])

        clw = sb("clw", [1, 3, D])
        cls4 = sb("cls4", [1, 4, 1])
        x1c = sb("x1c", [1, 2, D])
        XXc = sb("XXc", [P, 1])
        kv0t = sb("kv0t", [1, 2, D])
        k0 = sb("k0", [P, 1])
        c0s = sb("c0s", [P, 4])
        h1c = sb("h1c", [1, D])
        x2c = sb("x2c", [1, 2, D])
        x2cT = sb("x2cT", [P, 1])
        lgc = sb("lgc", [1, 1, NE])
        top8c = sb("top8c", [1, 1, 8])
        idx8c = sb("idx8c", [1, 1, 8], U32)
        idxfc = sb("idxfc", [1, 1, 2])
        gsmc = sb("gsmc", [1, 4, 1])
        eqc = sb("eqc", [1, 2, NE])
        gwc = sb("gwc", [1, 1, NE])
        gTc = sb("gTc", [NE, 1])
        gbc = sb("gbc", [P, NE])
        zc = sb("zc", [P, NE])
        hc = sb("hc", [P, NE])
        y3cl = sb("y3cl", [1, 4, D])

        A0 = psum("A0", [P, UT])
        A1 = psum("A1", [P, UT])
        B0 = psum("B0", [P, UT])
        T0 = psum("T0", [P, UT])
        zb = psum("zb", [P, 2, UT])
        yb = psum("yb", [P, 2, UT])

        (l_cst, l_par, l_wf, l_G, l_w1, l_w2, l_x, l_gate_lo, l_gate_hi) = [
            sem("loaded_" + n) for n in ("consts", "params", "folded", "timew", "w1", "w2", "x", "gates_lo", "gates_hi")]
        zeroed, ones_ok = sem("zeroed"), sem("ones_ok")
        fold_ps, fold_sb, fold_st, wfe_ok = sem("fold_ps"), sem("fold_sb"), sem("fold_stored"), sem("wfe_ok")
        mixf_ok, wmix_ok, G_ok = sem("mixf_ok"), sem("wmix_ok"), sem("G_ok")
        w1h_ok, w1l_ok = sem("w1h_ok"), sem("w1l_ok")
        uv_ps, u_done, v_done, h_ps, h_done = [sem(n) for n in ("uv_ps", "u_done", "v_done", "h_ps", "h_done")]
        x1_ps, xx_lo, xx_hi = sem("x1_ps"), sem("xx_lo"), sem("xx_hi")
        kv_ps, kt_clip, kt_exp, kv_done = [sem(n) for n in ("kv_ps", "kt_clip", "kt_exp", "kv_done")]
        kr_ps, kc_clip, kc_exp, er_done = [sem(n) for n in ("kr_ps", "kc_clip", "kc_exp", "er_done")]
        carry_ps, kinit_ok, sk_done, q_done, rq_done = [
            sem(n) for n in ("carry_ps", "kinit_ok", "sk_done", "q_done", "rq_done")]
        wkv_ps, wsum_done, rw_done, att_ps, h1_done = [
            sem(n) for n in ("wkv_ps", "wsum_done", "rw_done", "att_ps", "h1_done")]
        x2_ps, xs_hi, xs_lo = [sem(n) for n in ("x2_ps", "xs_hi", "xs_lo")]
        lg_ps, lg_done, top_done, idx_done = [sem(n) for n in ("lg_ps", "lg_done", "top_done", "idx_done")]
        idxf_done, gap_done, gexp, gden, g1_done, g2_done = [
            sem(n) for n in ("idxf_done", "gap_done", "gexp", "gden", "g1_done", "g2_done")]
        eq_done, eqg_done, gw_done = sem("eq_done"), sem("eqg_done"), sem("gw_done")
        gT_ps, gT_done, gT_stored, h1b_done = [sem(n) for n in ("gT_ps", "gT_done", "gT_stored", "h1b_done")]
        z_ps, relu_done, h_used = [sem(n) for n in ("z_ps", "relu_done", "h_used")]
        gated, prod_used, acc_done = [sem(n) for n in ("gated", "prod_used", "acc_done")]
        moe_ps, moe_read = sem("moe_ps"), sem("moe_read")
        settled = sem("settled")
        yg_done, fo_done, stored = sem("yg_done"), sem("fo_done"), sem("stored")

        def ln_sems(tag):
            return {n: sem(f"{tag}_{n}") for n in ("sum", "center", "square", "sumsq", "var", "rstd", "out")}

        ln1, ln2, ln3, lnc = ln_sems("ln1"), ln_sems("ln2"), ln_sems("ln3"), ln_sems("lnc")
        c_xT, c_xx, c_kv, c_clip, c_exp, c_kv0, c_C0, c_C0sb, c_q, c_rw, c_att, c_h1, c_x2T, c_x2sb, c_lg = [
            sem("cls_" + n) for n in ("xT", "xx", "kv", "clip", "exp", "kv0", "C0", "C0sb", "q", "rw", "att", "h1",
                                      "x2T", "x2sb", "lg")]
        c_gate, c_gexp, c_g, c_gT, c_gTsb, c_z, c_zb, c_h, c_moe, c_y, c_fin, c_fo, c_out = [
            sem("cls_" + n) for n in ("gate", "gexp", "g", "gT", "gTsb", "z", "zb", "h", "moe", "y", "fin", "fo",
                                      "out")]

        uv_v = uv[:, :].rearrange("p (v n) -> p n v", n=NPATCH)

        def tiles(bank):
            return bank[:, 0:NT * D].rearrange("p (i d) -> p i d", d=D)

        def reuse(eng, semaphore, value):
            if not (isinstance(value, int) and value <= 0):
                eng.wait_ge(semaphore, value)

        def settle(eng, semaphore, value):
            eng.wait_ge(semaphore, value)
            eng.sem_inc(settled, 1)

        def fill(a1, a2, cls):
            for step in FILL:
                if step[0] == "C":
                    cls(step[2])
                else:
                    (a1 if step[0] == "A1" else a2)(step[1], step[1], step[2])

        def run(a1, a2, m, u, c, with_a1, with_a2):
            for stage, step, *pair in WINDOW:
                if stage == "A1" and with_a1:
                    a1(u + 2, c, step)
                elif stage == "A2" and with_a2:
                    a2(u + 1, 1 - c, step)
                elif stage == "M" and pair == [NPAIR]:
                    if with_a2:
                        m(u + 1, 1 - c, step, 0)
                elif stage == "M":
                    m(u, c, step, pair[0] if pair else None)

        def windows(eng, a1, a2, m):
            with eng.Fori(0, NB - 1) as b:
                run(a1, a2, m, 2 * b, 0, True, True)
                run(a1, a2, m, 2 * b + 1, 1, True, True)
            run(a1, a2, m, NU - 2, 0, False, True)
            run(a1, a2, m, NU - 1, 1, False, False)

        def ln_center(dve, s, n, src, st, dst, p, t):
            dve.tensor_reduce(st[0:p, 0, :], src, AX_X, ALU.add).then_inc(s["sum"], 1)
            dve.wait_ge(s["sum"], n + 1)
            mean = st[0:p, 0, :].unsqueeze(2).broadcast_to([p, t, D])
            dve.scalar_tensor_tensor(dst, mean, -1.0 / D, src, ALU.mult, ALU.add).then_inc(s["center"], 1)

        def ln_square(act, s, n, src, dst):
            act.wait_ge(s["center"], n + 1)
            act.activation(dst, src, ACT.Square).then_inc(s["square"], 1)

        def ln_var(dve, s, n, sqr, st, p):
            dve.wait_ge(s["square"], n + 1)
            dve.tensor_reduce(st[0:p, 1, :], sqr, AX_X, ALU.add).then_inc(s["sumsq"], 1)
            dve.wait_ge(s["sumsq"], n + 1)
            dve.tensor_scalar(st[0:p, 2, :], st[0:p, 1, :], 1.0 / D, EPS, ALU.mult, ALU.add).then_inc(s["var"], 1)

        def ln_rstd(pool, s, n, st, p, t):
            pool.wait_ge(s["var"], n + 1)
            pool.tensor_tensor(st[0:p, 3, :], st[0:p, 2, :], mhalf[0:p, 0:t], ALU.pow).then_inc(s["rstd"], 1)

        def ln_scale(dve, s, n, src, st, dsts, p, t):
            dve.wait_ge(s["rstd"], n + 1)
            r = st[0:p, 3, :].unsqueeze(2).broadcast_to([p, t, D])
            for dst in dsts:
                last = dve.tensor_tensor(dst, src, r, ALU.mult)
            last.then_inc(s["out"], 1)

        block = ctx.enter_context(nc.Block())

        @block.sync
        def _(sp):
            def load_x(b):
                for half in range(2):
                    src = x[b].rearrange("c (m h q) v -> h c m (q v)", h=2, q=4)[half]
                    sp.dma_start(xt[D * half:D * half + D, :, :], src).then_inc(l_x, 16)

            def spread_gates(u, c):
                sp.wait_ge(gT_done, u + 1)
                sp.dma_start(spread[c], gT[:, c, :]).then_inc(gT_stored, 16)
                sp.wait_ge(gT_stored, 16 * u + 32)
                half = NPAIR // 2
                for part in range(2):
                    for k in range(2):
                        offset = (c * NE + NPAIR * part + k) * UT
                        src = bass.AP(spread.tensor, offset, [[0, D], [2 * UT, half], [1, UT]])
                        sp.dma_start(gbs[D * k:D * k + D, c, half * part:half * part + half, :],
                                     src).then_inc((l_gate_lo, l_gate_hi)[part], 16)

            def store(u, b, c):
                sp.wait_ge(fo_done, u + 2)
                dst = out[b, 1 + c * UT:1 + (c + 1) * UT, :].rearrange("(i p) d -> p i d", p=P)
                sp.dma_start(dst, fo[:, :, :]).then_inc(stored, 16)

            sp.dma_start(cst[:, :], consts).then_inc(l_cst, 16)
            sp.dma_start(par[:, :], small).then_inc(l_par, 16)
            load_x(0)
            sp.wait_ge(fold_sb, 2)
            sp.dma_start(folded.rearrange("(j a) -> j a", a=2 * UT), wfp[:, :]).then_inc(fold_st, 16)
            sp.dma_start(grev[:, :], bass.AP(time_row.tensor, 0, [[1, P], [1, KPAD + 1]])).then_inc(l_G, 16)
            sp.wait_ge(fold_st, 16)
            sp.dma_start(wf[:, :, :, :].rearrange("p q s o -> p (q s) o"),
                         folded.rearrange("(j p o) -> p j o", p=P, o=D)).then_inc(l_wf, 16)
            sp.dma_start(w1raw[:, :, :], w1).then_inc(l_w1, 16)
            sp.dma_start(w2s[:, :, :], w2).then_inc(l_w2, 16)
            sp.wait_ge(uv_ps, 4)
            load_x(1)
            spread_gates(0, 0)
            with sp.Fori(0, NB - 2) as b:
                spread_gates(2 * b + 1, 1)
                store(2 * b, b, 0)
                sp.wait_ge(uv_ps, 4 * b + 8)
                load_x(b + 2)
                spread_gates(2 * b + 2, 0)
                store(2 * b + 1, b, 1)
            for u in range(NU - 4, NU):
                if u + 1 < NU:
                    spread_gates(u + 1, (u + 1) % 2)
                store(u, u // 2, u % 2)
            sp.wait_ge(c_fo, 1)
            for b in range(NB):
                sp.dma_start(out[b, 0:1, :], y3cl[:, 3, :]).then_inc(c_out, 16)
            sp.wait_ge(stored, 16 * (NU + 1))
            sp.wait_ge(c_out, 16 * NB)

        @block.tensor
        def _(pe):
            mm = pe.matmul

            def turn(bank, src, done):
                for i in range(NT):
                    last = pe.transpose(bank[:, P * i:P * i + P], src[:, i, :, :], ident)
                last.then_inc(done, 1)

            def a1(u, c, step):
                if step == "embed":
                    reuse(pe, kc_clip, u)
                    reuse(pe, er_done, u)
                    if c == 0:
                        pe.wait_ge(l_x, 16 * u + 32)
                    for q in range(4):
                        last = mm(A0[:, :], wf[:, q, :, :], xt[:, :, VARS * q + UV * c:VARS * q + UV * c + UV],
                                  start=q == 0, stop=q == 3)
                    last.then_inc(uv_ps, 1)
                elif step == "edge":
                    reuse(pe, kinit_ok, u)
                    mm(A1[:, 0:UV], wfe[D:P, 0, :], xt[D:P, 15, 3 * VARS + UV * c:3 * VARS + UV * c + UV],
                       start=True, stop=True).then_inc(uv_ps, 1)
                elif step == "tokens":
                    pe.wait_ge(v_done, 2 * u + 2)
                    pe.wait_ge(u_done, u + 1)
                    for i in range(NT):
                        last = mm(A1[:, D * i:D * i + D], uv[:, P * i:P * i + P], dup2, start=True, stop=True)
                    last.then_inc(h_ps, 1)
                elif step == "turn":
                    pe.wait_ge(ln1["out"], u + 1)
                    turn(A0, x1, x1_ps)
                elif step == "kv":
                    pe.wait_ge(xx_lo, u + 1)
                    pe.wait_ge(xx_hi, u + 1)
                    for i in range(NT):
                        t = UT * c + P * i
                        last = mm(A1[:, P * i:P * i + P], XX[:, t:t + P], wmix[:, 0:2, :], start=True, stop=True)
                    last.then_inc(kv_ps, 1)
                elif step == "kr":
                    for i in range(2):
                        for half in range(2):
                            t = UT * c + Q * half
                            last = mm(A0[D * half:D * half + D, Q * i:Q * i + Q], wmix[:, 1 + i, :], XX[:, t:t + Q],
                                      start=True, stop=True)
                    last.then_inc(kr_ps, 1)
                elif step == "carry":
                    pe.wait_ge(kt_exp, u + 1)
                    pe.wait_ge(kv_done, u + 1)
                    for i in range(2):
                        last = mm(A1[D:P, 0:1], kt[:, i, :], ones[:, 0:1], start=i == 0, stop=i == 1)
                    last.then_inc(carry_ps, 1)

            def a2(u, c, step):
                if step == "wkv":
                    reuse(pe, gT_done, u)
                    pe.wait_ge(kv_done, u + 1)
                    n_src = 4 * c + 4
                    for j in range(n_src):
                        for half in range(2):
                            ahead = 2 * Q * c + Q * half - P * j
                            rows = slice(D * half, D * half + D)
                            n_half = n_src - 2 + 2 * half
                            if ahead >= 0:
                                last = mm(B0[rows, 0:Q], kv[:, j // NT, j % NT, :], G[:, ahead:ahead + Q],
                                          start=j == 0, stop=j == n_half - 1, skip_group_check=True)
                            elif ahead == -P:
                                last = mm(B0[rows, P:Q], kv[:, j // NT, j % NT, :], G[:, 0:P],
                                          start=False, stop=j == n_half - 1, skip_group_check=True)
                    last.then_inc(wkv_ps, 1)
                elif step == "att":
                    pe.wait_ge(rw_done, u + 1)
                    out_tiles = B0[:, 0:NT * D].rearrange("p (s i d) -> p s i d", s=2, i=2)
                    for i in range(2):
                        last = mm(out_tiles[:, :, i, :], rw[:, P * i:P * i + P], wobd, start=True, stop=True)
                    last.then_inc(att_ps, 1)
                elif step == "turn":
                    pe.wait_ge(ln2["out"], u + 1)
                    turn(B0, x2s[:, c, :, :, :], x2_ps)
                elif step == "logits":
                    pe.wait_ge(xs_lo, u + 1)
                    for i in range(NT):
                        last = mm(B0[:, NE * i:NE * i + NE], xs[:, c, P * i:P * i + P].bitcast(F32), gw2,
                                  start=True, stop=True)
                    last.then_inc(lg_ps, 1)
                elif step == "spread":
                    pe.wait_ge(gw_done, u + 1)
                    for i in range(NT):
                        last = pe.transpose(B0[0:NE, P * i:P * i + P], gw[:, i, :], ident)
                    last.then_inc(gT_ps, 1)

            def expert_in(u, c, p):
                for k in range(2):
                    e, n = 2 * p + k, 16 * u + 2 * p + k
                    pe.wait_ge(relu_done, n + 1)
                    mm(zb[:, k, :], w1h[:, e, :], xs[:, c, :], start=True, stop=False)
                    mm(zb[:, k, :], w1l[:, e, :], xs[:, c, :], start=False, stop=True).then_inc(z_ps, 1)

            def expert_out(u, c, p):
                n = NPAIR * u + p
                pe.wait_ge(relu_done, 2 * n + 4)
                pe.wait_ge(gated, n + 1)
                for k in range(2):
                    last = mm(yb[D * k:D * k + D, p % 2, :], w2s[:, 2 * p + k, :], hr[:, 2 * (p % 2) + k, :],
                              start=True, stop=True)
                last.then_inc(h_used, 1)

            def moe_tokens(u, c):
                pe.wait_ge(acc_done, u + 1)
                pe.wait_ge(moe_read, u + 1)
                for i in range(NT):
                    o = T0[:, D * i:D * i + D]
                    mm(o, acc[:, c, P * i:P * i + P], dup2, start=True, stop=False)
                    last = mm(o, gT[:, c, P * i:P * i + P], b2s, start=False, stop=True)
                last.then_inc(moe_ps, 1)

            def cls(step):
                zA, yA, yB = T0[:, :], yb[:, 0, :], yb[:, 1, :]
                if step == "mix":
                    pe.wait_ge(lnc["out"], 1)
                    pe.transpose(yB[:, 0:1], x1c[:, :, :], cst[0:1, C_ID:C_ID + 1]).then_inc(c_xT, 1)
                    pe.wait_ge(c_xx, 1)
                    pe.wait_ge(wmix_ok, 3)
                    mm(zA[0:1, 0:P], XXc[:, :], wmix[:, 0:2, :], start=True, stop=True)
                    for half in range(2):
                        for j in range(2):
                            last = mm(yA[D * half:D * half + D, j:j + 1], wmix[:, 1 + j, :], XXc[:, :],
                                      start=True, stop=True)
                    last.then_inc(c_kv, 1)
                    pe.wait_ge(c_kv0, 1)
                    pe.wait_ge(G_ok, 1)
                    for c in range(2):
                        for half in range(2):
                            t = 1 + UT * c + Q * half
                            mm(yB[D * half:D * half + D, Q * c:Q * c + Q], kv0t[:, 0, :], G[0:1, t:t + Q],
                               start=True, stop=True)
                    mm(yA[0:D, 2:3], kv0t[:, 0, :], G[0:1, 0:1], start=True, stop=True).then_inc(c_C0, 1)
                elif step == "norm":
                    pe.wait_ge(c_rw, 1)
                    mm(zA[0:1, 0:D], c0s[0:D, 3:4], par[0:D, S_WO:S_WO + D], start=True, stop=True).then_inc(c_att, 1)
                    pe.wait_ge(l_wf, 16)
                elif step == "edge":
                    pe.wait_ge(wfe_ok, 3)
                elif step == "turn":
                    pe.wait_ge(lnc["out"], 2)
                    pe.wait_ge(c_C0sb, 1)
                    pe.transpose(yB[:, 0:1], x2c[:, :, :], cst[0:1, C_ID:C_ID + 1]).then_inc(c_x2T, 1)
                    pe.wait_ge(c_x2sb, 1)
                    mm(yB[0:1, 0:NE], x2cT[0:D, :], par[0:D, S_GW:S_GW + NE], start=True, stop=True).then_inc(c_lg, 1)
                elif step in ("z0", "z1"):
                    pe.wait_ge(l_w1, 16)
                    for e in range(NPAIR * int(step[1]), NPAIR * int(step[1]) + NPAIR):
                        last = mm(yA[:, e:e + 1], w1raw[0:D, e, :], x2cT[0:D, :], start=True, stop=True)
                    last.then_inc(c_z, 1)
                elif step == "spread":
                    pe.wait_ge(c_g, 4)
                    mm(yB[:, 0:NE], ones[0:1, 0:P], gwc[:, 0, :], start=True, stop=True)
                    pe.transpose(yB[0:NE, NE:NE + 1], gwc[:, 0, :], cst[0:1, C_ID:C_ID + 1]).then_inc(c_gT, 1)
                elif step == "experts":
                    pe.wait_ge(w1l_ok, 1)
                    expert_in(0, 0, 0)
                elif step == "y0":
                    pe.wait_ge(c_gTsb, 1)
                    pe.wait_ge(c_h, 1)
                    pe.wait_ge(l_w2, 16)
                    mm(zA[0:1, 0:D], gTc[:, :], b2s, start=True, stop=False)
                    for e in range(NPAIR):
                        mm(zA[0:1, 0:D], hc[:, e:e + 1], w2s[:, e, :], start=False, stop=False)
                elif step == "y1":
                    for e in range(NPAIR, NE):
                        last = mm(zA[0:1, 0:D], hc[:, e:e + 1], w2s[:, e, :], start=False, stop=e == NE - 1)
                    last.then_inc(c_moe, 1)

            pe.wait_ge(l_cst, 16)
            for i in range(2):
                t = C_TOKW + UT * i
                mm((A0, A1)[i][0:D, :], cst[:, C_DFT:C_DFT + D], cst[:, t:t + UT],
                   start=True, stop=True).then_inc(fold_ps, 1)
            pe.wait_ge(fold_sb, 2)
            pe.wait_ge(l_par, 16)
            pe.wait_ge(ones_ok, 1)
            fill(a1, a2, cls)

            def m(u, c, step, p):
                if step == "in":
                    expert_in(u, c, p)
                elif step == "out":
                    expert_out(u, c, p)
                elif step == "tokens":
                    moe_tokens(u, c)

            windows(pe, a1, a2, m)

        @block.scalar
        def _(act):
            fn = act.activation

            def a1(u, c, step):
                if step == "edge":
                    act.wait_ge(uv_ps, 2 * u + 1)
                    fn(uv_v[0:D, :, :], A0[0:D, :].rearrange("p (m v) -> p m v", v=UV), ACT.Copy).then_inc(u_done, 1)
                elif step == "tokens":
                    reuse(act, h1_done, u - 1)
                    act.wait_ge(h_ps, u + 1)
                    fn(h[:, c, :, :], tiles(A1), ACT.Copy).then_inc(h_done, 1)
                elif step == "var":
                    ln_square(act, ln1, u, xc1[:, :, :], sq1[:, :, :])
                elif step == "turn":
                    act.wait_ge(x1_ps, u + 1)
                    fn(XX[0:D, UT * c:UT * c + UT], A0[0:D, :], ACT.Copy).then_inc(xx_lo, 1)
                elif step == "kv":
                    act.wait_ge(kt_clip, u + 1)
                    fn(kt[:, :, :], kt[:, :, :], ACT.Exp).then_inc(kt_exp, 1)
                elif step == "kr":
                    act.wait_ge(kc_clip, u + 1)
                    fn(kc[:, :], kc[:, :], ACT.Exp).then_inc(kc_exp, 1)
                    fn(er[:, :], A0[:, Q:2 * Q], ACT.Exp, scale=-1.0).then_inc(er_done, 1)

            def a2(u, c, step):
                if step == "var":
                    ln_square(act, ln2, u, xc2[:, :, :], sq2[:, :, :])
                elif step == "turn":
                    act.wait_ge(x2_ps, u + 1)
                    fn(xs[:, c, :], B0[:, :], ACT.Copy).then_inc(xs_hi, 1)
                elif step == "gates":
                    act.wait_ge(gap_done, u + 1)
                    fn(gsm[:, 1, :], gsm[:, 0, :], ACT.Exp).then_inc(gexp, 1)
                elif step == "spread":
                    reuse(act, gT_stored, 16 * u)
                    act.wait_ge(gT_ps, u + 1)
                    fn(gT[:, c, :], B0[0:NE, :], ACT.Copy).then_inc(gT_done, 1)

            def relu(u, p):
                n = NPAIR * u + p
                act.wait_ge(h_used, n + 1)
                for k in range(2):
                    act.wait_ge(z_ps, 2 * n + k + 1)
                    fn(hr[:, 2 * (p % 2) + k, :], zb[:, k, :], ACT.Relu,
                       bias=b1T[:, 2 * p + k:2 * p + k + 1]).then_inc(relu_done, 1)

            def cls(step):
                zA, yA, yB = T0[:, :], yb[:, 0, :], yb[:, 1, :]
                if step == "mix":
                    act.wait_ge(c_xT, 1)
                    fn(XX[D:P, 0:1], yB[D:P, 0:1], ACT.Copy)
                    act.wait_ge(zeroed, 3)
                    fn(XXc[0:D, :], yB[0:D, 0:1], ACT.Copy).then_inc(c_xx, 1)
                    act.wait_ge(c_clip, 2)
                    fn(kv0t[:, 1, :], kv0t[:, 1, :], ACT.Exp)
                    fn(k0[:, :], k0[:, :], ACT.Exp)
                    fn(c0s[:, 0:1], yA[:, 1:2], ACT.Exp, scale=-1.0).then_inc(c_exp, 1)
                    act.wait_ge(c_C0, 1)
                    fn(C0[:, :, :], yB.rearrange("p (c t) -> p c t", c=2), ACT.Copy).then_inc(c_C0sb, 1)
                elif step == "norm":
                    ln_square(act, lnc, 1, clw[:, 0:1, :], clw[:, 1:2, :])
                elif step == "turn":
                    act.wait_ge(c_x2T, 1)
                    fn(x2cT[:, :], yB[:, 0:1], ACT.Copy).then_inc(c_x2sb, 1)
                elif step == "gates":
                    act.wait_ge(c_gate, 4)
                    fn(gsmc[:, 1, :], gsmc[:, 0, :], ACT.Exp).then_inc(c_gexp, 1)
                elif step == "w1":
                    act.wait_ge(l_w1, 16)
                    fn(w1h[:, :, :], w1raw[:, :, :], ACT.Copy).then_inc(w1h_ok, 1)
                elif step == "spread":
                    act.wait_ge(c_gT, 1)
                    fn(gTc[:, :], yB[0:NE, NE:NE + 1], ACT.Copy)
                    fn(gbc[:, :], yB[:, 0:NE], ACT.Copy).then_inc(c_gTsb, 1)
                elif step == "experts":
                    relu(0, 0)
                elif step == "out":
                    ln_square(act, lnc, 2, y3cl[:, 1:2, :], y3cl[:, 2:3, :])

            act.wait_ge(fold_ps, 1)
            fn(wfp[:, 0:UT], A0[0:D, :], ACT.Copy).then_inc(fold_sb, 1)
            act.wait_ge(l_par, 16)
            ln_square(act, lnc, 0, clw[:, 0:1, :], clw[:, 1:2, :])
            fill(a1, a2, cls)

            def m(u, c, step, p):
                if step == "in":
                    relu(u, p)
                elif step == "var":
                    ln_square(act, ln3, u, y3c[:, :, :], y3q[:, :, :])

            windows(act, a1, a2, m)

        @block.vector
        def _(dve):
            tt, ts, stt = dve.tensor_tensor, dve.tensor_scalar, dve.scalar_tensor_tensor

            def gate_top(lgt, top, idx, n_tiles, n0, s_top, s_idx):
                for i in range(n_tiles):
                    dve.max(top[:, i, :], lgt[:, i, :]).then_inc(s_top, 1)
                for i in range(n_tiles):
                    settle(dve, s_top, n0 + i + 1)
                    dve.max_index(idx[:, i, :], top[:, i, :], lgt[:, i, :]).then_inc(s_idx, 1)

            def a1(u, c, step):
                if step == "edge":
                    dve.wait_ge(uv_ps, 2 * u + 1)
                    dve.tensor_copy(uv_v[D:P, 0:15, :],
                                    A0[D:P, UV:].rearrange("p (m v) -> p m v", v=UV)).then_inc(v_done, 1)
                    dve.wait_ge(uv_ps, 2 * u + 2)
                    dve.tensor_copy(uv_v[D:P, 15, :], A1[D:P, 0:UV]).then_inc(v_done, 1)
                elif step == "tokens":
                    dve.wait_ge(h_done, u + 1)
                    ln_center(dve, ln1, u, h[:, c, :, :], st1, xc1[:, :, :], P, NT)
                elif step == "var":
                    ln_var(dve, ln1, u, sq1[:, :, :], st1, P)
                elif step == "scale":
                    ln_scale(dve, ln1, u, xc1[:, :, :], st1, [x1[:, :, 0, :], x1[:, :, 1, :]], P, NT)
                elif step == "turn":
                    dve.wait_ge(x1_ps, u + 1)
                    dve.tensor_copy(XX[D:P, 1 + UT * c:1 + UT * c + UT], A0[D:P, :]).then_inc(xx_hi, 1)
                elif step == "kv":
                    bank = A1[:, :].rearrange("p (i w d) -> p i w d", i=NT, w=2)
                    dve.wait_ge(kv_ps, u + 1)
                    ts(kt[:, :, :], bank[:, :, 1, :], -60.0, 30.0, ALU.max, ALU.min).then_inc(kt_clip, 1)
                    dve.wait_ge(kt_exp, u + 1)
                    tt(kv[:, c, :, :], kt[:, :, :], bank[:, :, 0, :], ALU.mult).then_inc(kv_done, 1)
                elif step == "kr":
                    dve.wait_ge(kr_ps, u + 1)
                    ts(kc[:, :], A0[:, 0:Q], -60.0, 30.0, ALU.max, ALU.min).then_inc(kc_clip, 1)
                elif step == "carry":
                    dve.wait_ge(carry_ps, u + 1)
                    before = k0[D:P, :] if c == 0 else sk[D:P, 0, Q - 1:Q]
                    if c == 1:
                        dve.tensor_copy(kinit[0:D, 1:2], sk[D:P, 0, Q - 1:Q])
                    tt(kinit[D:P, c:c + 1], A1[D:P, 0:1], before, ALU.add).then_inc(kinit_ok, 1)
                    dve.wait_ge(kinit_ok, u + 1)
                    dve.wait_ge(kc_exp, u + 1)
                    dve.tensor_tensor_scan(sk[:, c, :], ones[:, :], kc[:, :], kinit[:, c:c + 1], ALU.mult,
                                           ALU.add).then_inc(sk_done, 1)
                    dve.wait_ge(sk_done, u + 1)
                    dve.wait_ge(er_done, u + 1)
                    stt(er[:, :], er[:, :], 1.0, sk[:, c, :], ALU.add, ALU.mult).then_inc(q_done, 1)
                elif step == "rq":
                    dve.wait_ge(q_done, u + 1)
                    dve.reciprocal(rq[:, :], er[:, :]).then_inc(rq_done, 1)

            def a2(u, c, step):
                if step == "wkv":
                    dve.wait_ge(wkv_ps, u + 1)
                    tt(wsum[:, :], B0[:, 0:Q], C0[:, c, :], ALU.add).then_inc(wsum_done, 1)
                    dve.wait_ge(wsum_done, u + 1)
                    dve.wait_ge(rq_done, u + 1)
                    tt(rw[:, :], wsum[:, :], rq[:, :], ALU.mult).then_inc(rw_done, 1)
                elif step == "att":
                    reuse(dve, h1b_done, u)
                    dve.wait_ge(att_ps, u + 1)
                    tt(h1[:, :, :], tiles(B0), h[:, c, :, :], ALU.add).then_inc(h1_done, 1)
                    settle(dve, h1_done, u + 1)
                    ln_center(dve, ln2, u, h1[:, :, :], st2, xc2[:, :, :], P, NT)
                elif step == "var":
                    ln_var(dve, ln2, u, sq2[:, :, :], st2, P)
                elif step == "scale":
                    ln_scale(dve, ln2, u, xc2[:, :, :], st2, [x2s[:, c, :, 0, :], x2s[:, c, :, 1, :]], P, NT)
                elif step == "turn":
                    lo = xs[D:P, c, :]
                    dve.wait_ge(xs_hi, u + 1)
                    tt(lo, B0[D:P, :], lo.bitcast(F32), ALU.subtract).then_inc(xs_lo, 1)
                elif step == "logits":
                    dve.wait_ge(lg_ps, u + 1)
                    tt(lg[:, :, :], B0[:, 0:NT * NE].rearrange("p (i e) -> p i e", e=NE),
                       gbb.unsqueeze(1).broadcast_to([P, NT, NE]), ALU.add).then_inc(lg_done, 1)
                    settle(dve, lg_done, u + 1)
                    gate_top(lg, top8, idx8, NT, NT * u, top_done, idx_done)
                    tt(gsm[:, 0, :], top8[:, :, 1], top8[:, :, 0], ALU.subtract).then_inc(gap_done, 1)
                    dve.wait_ge(idx_done, NT * u + NT)
                    dve.tensor_copy(idxf[:, :, :], idx8[:, :, 0:2]).then_inc(idxf_done, 1)
                elif step == "gates":
                    dve.wait_ge(idxf_done, u + 1)
                    for k, row in enumerate((eq1, eq2)):
                        tt(row[:, :, :], iota[:, :].unsqueeze(1).broadcast_to([P, NT, NE]),
                           idxf[:, :, k:k + 1].broadcast_to([P, NT, NE]), ALU.is_equal).then_inc(eq_done, 1)
                    dve.wait_ge(gexp, u + 1)
                    ts(gsm[:, 2, :], gsm[:, 1, :], 1.0, None, ALU.add).then_inc(gden, 1)
                    dve.wait_ge(gden, u + 1)
                    dve.reciprocal(gsm[:, 3, :], gsm[:, 2, :]).then_inc(g1_done, 1)
                    dve.wait_ge(g1_done, u + 1)
                    tt(gsm[:, 2, :], gsm[:, 1, :], gsm[:, 3, :], ALU.mult).then_inc(g2_done, 1)
                    dve.wait_ge(eq_done, 2 * u + 2)
                    dve.wait_ge(g2_done, u + 1)
                    for row, w in ((eq1, gsm[:, 3, :]), (eq2, gsm[:, 2, :])):
                        last = tt(row[:, :, :], row[:, :, :], w.unsqueeze(2).broadcast_to([P, NT, NE]), ALU.mult)
                    last.then_inc(eqg_done, 1)
                    dve.wait_ge(eqg_done, u + 1)
                    tt(gw[:, :, :], eq1[:, :, :], eq2[:, :, :], ALU.add).then_inc(gw_done, 1)

            def gate(u, c, p):
                n = NPAIR * u + p
                dve.wait_ge(h_used, n + 3)
                if p == 0:
                    dve.wait_ge(l_gate_lo, 32 * u + 32)
                    dve.wait_ge(moe_ps, u + 1)
                if p == NPAIR // 2:
                    dve.wait_ge(l_gate_hi, 32 * u + 32)
                if p > 0:
                    m = (NPAIR - 1) * u + p - 1
                    dve.wait_ge(prod_used, m + 1)
                dst = acc[:, c, :] if p == 0 else prod[:, p % 2, :]
                tt(dst, yb[:, p % 2, :], gbs[:, c, p, :], ALU.mult).then_inc(gated, 1)

            def cls(step):
                zA, yA, yB = T0[:, :], yb[:, 0, :], yb[:, 1, :]
                if step == "mix":
                    dve.wait_ge(c_kv, 1)
                    ts(kv0t[:, 1, :], zA[0:1, D:P], -60.0, 30.0, ALU.max, ALU.min).then_inc(c_clip, 1)
                    ts(k0[:, :], yA[:, 0:1], -60.0, 30.0, ALU.max, ALU.min).then_inc(c_clip, 1)
                    dve.wait_ge(c_exp, 1)
                    tt(kv0t[:, 0, :], kv0t[:, 1, :], zA[0:1, 0:D], ALU.mult).then_inc(c_kv0, 1)
                    dve.tensor_copy(kinit[0:D, 0:1], k0[0:D, :])
                    stt(c0s[:, 1:2], c0s[:, 0:1], 1.0, k0[:, :], ALU.add, ALU.mult).then_inc(c_q, 1)
                    dve.wait_ge(c_q, 1)
                    dve.reciprocal(c0s[:, 2:3], c0s[:, 1:2]).then_inc(c_q, 1)
                elif step == "edge":
                    dve.wait_ge(l_wf, 16)
                    dve.tensor_reduce(wfe[:, 1, :], wf[:, :, :, :].rearrange("p q s o -> p (s o) q"), AX_X,
                                      ALU.add).then_inc(wfe_ok, 1)
                    dve.wait_ge(wfe_ok, 1)
                    dve.tensor_copy(wfe[D:P, 2, :], wfe[0:D, 1, :]).then_inc(wfe_ok, 1)
                    dve.wait_ge(wfe_ok, 2)
                    tt(wfe[D:P, 0, :], wfe[D:P, 1, :], wfe[D:P, 2, :], ALU.add).then_inc(wfe_ok, 1)
                elif step == "norm":
                    dve.wait_ge(c_q, 2)
                    dve.wait_ge(c_C0, 1)
                    tt(c0s[0:D, 3:4], yA[0:D, 2:3], c0s[0:D, 2:3], ALU.mult).then_inc(c_rw, 1)
                    dve.wait_ge(c_att, 1)
                    tt(h1c[:, :], zA[0:1, 0:D], cl, ALU.add).then_inc(c_h1, 1)
                    dve.wait_ge(c_h1, 1)
                    ln_center(dve, lnc, 1, h1c[:, :].unsqueeze(1), cls4, clw[:, 0:1, :], 1, 1)
                    ln_var(dve, lnc, 1, clw[:, 1:2, :], cls4, 1)
                    ln_scale(dve, lnc, 1, clw[:, 0:1, :], cls4, [x2c[:, 0:1, :], x2c[:, 1:2, :]], 1, 1)
                elif step == "gates":
                    dve.wait_ge(c_lg, 1)
                    tt(lgc[:, 0, :], yB[0:1, 0:NE], par[0:1, S_GB:S_GB + NE], ALU.add).then_inc(c_gate, 1)
                    dve.wait_ge(c_gate, 1)
                    gate_top(lgc, top8c, idx8c, 1, 1, c_gate, c_gate)
                    tt(gsmc[:, 0, :], top8c[:, :, 1], top8c[:, :, 0], ALU.subtract).then_inc(c_gate, 1)
                    dve.wait_ge(c_gate, 4)
                    dve.tensor_copy(idxfc[:, :, :], idx8c[:, :, 0:2]).then_inc(c_gate, 1)
                    dve.wait_ge(c_gate, 5)
                    for k in range(2):
                        ts(eqc[:, k, :], iota[0:1, :], idxfc[:, 0, k:k + 1], None, ALU.is_equal)
                    dve.wait_ge(c_gexp, 1)
                    ts(gsmc[:, 2, :], gsmc[:, 1, :], 1.0, None, ALU.add).then_inc(c_g, 1)
                    dve.wait_ge(c_g, 1)
                    dve.reciprocal(gsmc[:, 3, :], gsmc[:, 2, :]).then_inc(c_g, 1)
                    dve.wait_ge(c_g, 2)
                    tt(gsmc[:, 2, :], gsmc[:, 1, :], gsmc[:, 3, :], ALU.mult)
                    ts(gwc[:, 0, :], eqc[:, 0, :], gsmc[:, 3, :], None, ALU.mult).then_inc(c_g, 1)
                    dve.wait_ge(c_g, 3)
                    stt(gwc[:, 0, :], eqc[:, 1, :], gsmc[:, 2, :], gwc[:, 0, :], ALU.mult, ALU.add).then_inc(c_g, 1)
                elif step == "spread":
                    dve.wait_ge(c_z, 2)
                    tt(zc[:, :], yA[:, 0:NE], b1T, ALU.add).then_inc(c_zb, 1)
                    dve.wait_ge(c_zb, 1)
                    dve.wait_ge(c_gTsb, 1)
                    stt(hc[:, :], zc[:, :], 0.0, gbc[:, :], ALU.max, ALU.mult).then_inc(c_h, 1)
                elif step == "out":
                    dve.wait_ge(c_moe, 1)
                    tt(y3cl[:, 0, :], zA[0:1, 0:D], x2c[:, 0, :], ALU.add).then_inc(c_y, 1)
                    dve.wait_ge(c_y, 1)
                    ln_center(dve, lnc, 2, y3cl[:, 0:1, :], cls4, y3cl[:, 1:2, :], 1, 1)
                    ln_var(dve, lnc, 2, y3cl[:, 2:3, :], cls4, 1)
                    ln_scale(dve, lnc, 2, y3cl[:, 1:2, :], cls4, [y3cl[:, 0:1, :]], 1, 1)
                    dve.wait_ge(lnc["out"], 3)
                    tt(y3cl[:, 1, :], y3cl[:, 0, :], par[0:1, S_GAM:S_GAM + D], ALU.mult).then_inc(c_fin, 1)
                    dve.wait_ge(c_fin, 1)
                    tt(y3cl[:, 2, :], y3cl[:, 1, :], par[0:1, S_BET:S_BET + D], ALU.add).then_inc(c_fin, 1)
                    dve.wait_ge(c_fin, 2)
                    tt(y3cl[:, 3, :], y3cl[:, 2, :], h1c[:, :], ALU.add).then_inc(c_fo, 1)

            dve.memset(ones[:, :], 1.0).then_inc(ones_ok, 1)
            dve.wait_ge(fold_ps, 2)
            dve.tensor_copy(wfp[:, UT:2 * UT], A1[0:D, :]).then_inc(fold_sb, 1)
            dve.wait_ge(l_par, 16)
            mix_hi = par[D:P, S_MIX:S_MIX + 3]
            ts(mix_hi, mix_hi, -1.0, 1.0, ALU.mult, ALU.add).then_inc(mixf_ok, 1)
            ln_center(dve, lnc, 0, cl.unsqueeze(1), cls4, clw[:, 0:1, :], 1, 1)
            dve.wait_ge(mixf_ok, 1)
            for i in range(3):
                ts(wmix[:, i, :], par[:, S_W + D * i:S_W + D * i + D], par[:, S_MIX + i:S_MIX + i + 1], None,
                   ALU.mult).then_inc(wmix_ok, 1)
            ln_var(dve, lnc, 0, clw[:, 1:2, :], cls4, 1)
            ln_scale(dve, lnc, 0, clw[:, 0:1, :], cls4, [x1c[:, 0:1, :], x1c[:, 1:2, :]], 1, 1)
            dve.wait_ge(zeroed, 3)
            dve.wait_ge(l_G, 16)
            dve.tensor_copy(G[:, :], grev[:, ::-1]).then_inc(G_ok, 1)
            fill(a1, a2, cls)

            def m(u, c, step, p):
                if step == "out":
                    gate(u, c, p)
                elif step == "center":
                    dve.wait_ge(moe_ps, u + 3)
                    tt(y3[:, :, :], tiles(T0), x2s[:, c, :, 0, :], ALU.add).then_inc(moe_read, 1)
                    dve.wait_ge(moe_read, u + 2)
                    ln_center(dve, ln3, u, y3[:, :, :], st3, y3c[:, :, :], P, NT)
                elif step == "var":
                    ln_var(dve, ln3, u, y3q[:, :, :], st3, P)
                elif step == "scale":
                    dve.wait_ge(yg_done, u + 1)
                    ln_scale(dve, ln3, u, y3c[:, :, :], st3, [yn[:, :, :]], P, NT)

            windows(dve, a1, a2, m)

        @block.gpsimd
        def _(pool):
            def a1(u, c, step):
                if step == "var":
                    ln_rstd(pool, ln1, u, st1, P, NT)

            def a2(u, c, step):
                if step == "var":
                    ln_rstd(pool, ln2, u, st2, P, NT)
                    reuse(pool, fo_done, u)
                    pool.tensor_tensor(h1b[:, c, :, :], h1[:, :, :], bet.unsqueeze(1).broadcast_to([P, NT, D]),
                                       ALU.add).then_inc(h1b_done, 1)

            def add_pair(u, c, p):
                n = NPAIR * u + p
                m = (NPAIR - 1) * u + p - 1
                pool.wait_ge(gated, n + 3)
                pool.wait_ge(prod_used, m + 2)
                last = pool.tensor_tensor(acc[:, c, :], acc[:, c, :], prod[:, p % 2, :], ALU.add)
                last.then_inc(prod_used, 1)
                if p == NPAIR - 1:
                    pool.wait_ge(prod_used, m + 3)
                    pool.sem_inc(acc_done, 1)

            def finish(u, c):
                ln_rstd(pool, ln3, u, st3, P, NT)
                pool.wait_ge(ln3["out"], u + 1)
                pool.tensor_tensor(yg[:, :, :], yn[:, :, :], gam.unsqueeze(1).broadcast_to([P, NT, D]),
                                   ALU.mult).then_inc(yg_done, 1)
                pool.wait_ge(yg_done, u + 2)
                pool.wait_ge(stored, 16 * u + 16)
                pool.tensor_tensor(fo[:, :, :], yg[:, :, :], h1b[:, c, :, :], ALU.add).then_inc(fo_done, 1)

            def cls(step):
                if step == "norm":
                    ln_rstd(pool, lnc, 1, cls4, 1, 1)
                elif step == "w1":
                    pool.wait_ge(w1h_ok, 1)
                    pool.tensor_tensor(w1l[:, :, :], w1raw[:, :, :], w1h[:, :, :].bitcast(F32),
                                       ALU.subtract).then_inc(w1l_ok, 1)
                elif step == "out":
                    ln_rstd(pool, lnc, 2, cls4, 1, 1)

            for i, (counter, free) in enumerate(((relu_done, 2), (gated, 2), (h_used, 2), (prod_used, 2), (moe_ps, 2),
                                                 (moe_read, 1), (yg_done, 1), (stored, 16), (fo_done, 1), (gT_stored, 16))):
                pool.memset(spare[:, i:i + 1], 0.0).then_inc(counter, free)
            pool.memset(mhalf[:, :], -0.5).then_inc(zeroed, 1)
            pool.memset(XXc[:, :], 0.0).then_inc(zeroed, 1)
            pool.iota(iota[:, :], [[1, NE]], base=0, channel_multiplier=0,
                      allow_small_or_imprecise_dtypes=True).then_inc(zeroed, 1)
            pool.wait_ge(zeroed, 3)
            ln_rstd(pool, lnc, 0, cls4, 1, 1)
            pool.wait_ge(l_par, 16)
            fill(a1, a2, cls)

            def m(u, c, step, p):
                if step == "out" and p > 0:
                    add_pair(u, c, p)
                elif step == "var":
                    finish(u, c)

            windows(pool, a1, a2, m)


def _consts(np, tok_W):
    c = np.zeros((P, C_END), np.float32)
    c[:, C_ID:C_ID + P] = np.eye(P)
    c[:, C_DUP:C_DUP + D] = np.tile(np.eye(D), (2, 1))
    angle = 2 * np.pi * np.arange(9)[:, None] * np.arange(16)[None, :] / 16
    dft = np.concatenate([np.cos(angle), -np.sin(angle)]) / 4
    by_group = c[:, C_DFT:C_DFT + D].reshape(4, 32, 4, 2, 2, 4)
    w = c[:, C_TOKW:].reshape(4, 32, 16, D)
    for g in range(4):
        by_group[g, 0:18, :, :, :, g] = dft.reshape(18, 2, 2, 4).transpose(0, 3, 1, 2)
        w[g, 0:18] = tok_W.reshape(D, 18, 4, 16)[:, :, g].transpose(1, 2, 0)
        c[32 * g:32 * g + 32, C_DFT:C_DFT + D] = by_group[g].reshape(32, D)
        c[32 * g:32 * g + 32, C_TOKW:] = w[g].reshape(32, 16 * D)
    return c


def _small(np, a):
    s = np.zeros((P, S_END), np.float32)
    for i, n in enumerate("vkr"):
        s[:, S_W + D * i:S_W + D * i + D] = np.tile(a[f"L0_attn_W{n}"], (2, 1))
        s[:, S_MIX + i] = np.tile(a[f"L0_attn_time_mix_{n}"].reshape(D), 2)
    for half in range(2):
        s[D * half:D * half + D, S_WO + D * half:S_WO + D * half + D] = a["L0_attn_Wo"]
    s[:, S_GW:S_GW + NE] = np.tile(a["L0_ffn_gate_w"], (2, 1))
    s[:, S_GB:S_GB + NE] = a["L0_ffn_gate_b"]
    s[:, S_GAM:S_GAM + D] = a["L0_ffn_gamma"]
    s[:, S_BET:S_BET + D] = a["L0_ffn_beta"]
    s[:, S_B1:S_B1 + NE] = a["L0_ffn_b1"].T
    s[0:NE, S_B2:S_B2 + D] = a["L0_ffn_b2"]
    s[0, S_CLS:S_CLS + D] = a["cls_tok"].reshape(D)
    return s


def kernel(**inputs):
    import numpy as _np
    import concourse.bacc as _bacc
    from concourse.bass_utils import run_bass_kernel_spmd as _run

    a = {name: _np.asarray(v) for name, v in inputs.items()}
    time_w = a["L0_attn_time_w"]
    row = _np.concatenate([_np.repeat(time_w[0:1], KPAD + 1 - WLEN), time_w, _np.zeros(P, _np.float32)])
    arrays = {
        "in_x": a["x"],
        "in_time_row": row,
        "in_w1": _np.tile(a["L0_ffn_w1"].transpose(1, 0, 2), (2, 1, 1)),
        "in_w2": a["L0_ffn_w2"].transpose(1, 0, 2),
        "in_consts": _consts(_np, a["L0_tok_W"]),
        "in_small": _small(_np, a),
    }
    arrays = {name: _np.ascontiguousarray(v) for name, v in arrays.items()}
    nc = _bacc.Bacc("TRN2", target_bir_lowering=False, num_devices=1)
    args = [nc.dram_tensor(name, v.shape, mybir.dt.from_np(v.dtype), kind="ExternalInput").ap()
            for name, v in arrays.items()]
    args.append(nc.dram_tensor("folded_weights", (P * 8 * D,), F32, kind="Internal").ap())
    args.append(nc.dram_tensor("router_weights", (2, NE, UT), F32, kind="Internal").ap())
    args.append(nc.dram_tensor("out_tokens", (NB, TOK + 1, D), F32, kind="ExternalOutput").ap())
    build(nc, *args)
    r = _run(nc, [arrays], core_ids=[0])
    return r.results[0]["out_tokens"]
```

```python
from contextlib import ExitStack

import concourse.bass as bass
from concourse import mybir

F32 = mybir.dt.float32
F32R = mybir.dt.float32r
U32 = mybir.dt.uint32
ALU = mybir.AluOpType
ACT = mybir.ActivationFunctionType
AX_X = mybir.AxisListType.X

P = 128
D = 64
NB = 4
VARS = 64
UV = VARS // 2
NPATCH = 16
TOK = VARS * NPATCH
UT = TOK // 2
NT = UT // P
Q = UT // 2
NU = 2 * NB
NE = 16
NPAIR = NE // 2
FF = 128
WLEN = 512
KPAD = 1024
EPS = 1e-5
C_ID, C_DFT, C_TOKW, C_END = 0, 128, 192, 1216
S_W, S_MIX, S_WO, S_GW, S_GB, S_GAM, S_BET, S_B1, S_B2, S_CLS, S_B2C, S_END = (
    0, 192, 195, 323, 339, 355, 419, 483, 499, 563, 627, 635)

WINDOW = (
    ("M", "in", 1), ("A1", "embed"), ("A2", "wkv"), ("M", "out", 0), ("M", "out", 1),
    ("M", "in", 2), ("A1", "edge"), ("A2", "att"),
    ("M", "in", 3), ("C", "out"), ("A2", "var"), ("A1", "tokens"), ("M", "out", 2),
    ("M", "in", 4), ("A2", "scale"), ("A1", "var"), ("M", "out", 3),
    ("M", "in", 5), ("M", "out", 4), ("A2", "turn"), ("A1", "scale"),
    ("M", "in", 6), ("M", "out", 5), ("A2", "logits"), ("A1", "turn"),
    ("M", "in", 7), ("M", "out", 6), ("A2", "gates"),
    ("M", "in", 8), ("M", "out", 7), ("A1", "kv"), ("A2", "spread"), ("A1", "kr"), ("M", "tokens"), ("M", "center"),
    ("A1", "carry"), ("M", "var"), ("A1", "rq"), ("M", "scale"),
)
FILL = (
    ("A1", 0, "embed"), ("C", 0, "edge"), ("C", 0, "x"), ("C", 0, "kv"), ("A1", 0, "edge"), ("A1", 0, "tokens"),
    ("A1", 0, "var"), ("C", 0, "c0"), ("C", 0, "att"), ("A1", 0, "scale"), ("A1", 0, "turn"), ("C", 0, "norm"),
    ("A1", 0, "kv"), ("A1", 0, "kr"), ("C", 0, "turn"), ("A1", 0, "carry"), ("C", 0, "z0"), ("C", 0, "gates"),
    ("A1", 0, "rq"), ("A2", 0, "wkv"), ("C", 0, "z1"), ("A2", 0, "att"), ("C", 0, "w1"), ("A1", 1, "embed"),
    ("A2", 0, "var"), ("A2", 0, "scale"), ("A2", 0, "turn"), ("C", 0, "spread"), ("A1", 1, "edge"),
    ("A2", 0, "logits"), ("A1", 1, "tokens"), ("A1", 1, "var"), ("C", 0, "y0"), ("C", 0, "y1"), ("A2", 0, "gates"),
    ("A1", 1, "scale"), ("A1", 1, "turn"), ("C", 0, "experts"), ("A2", 0, "spread"), ("A1", 1, "kv"),
    ("A1", 1, "kr"), ("A1", 1, "carry"), ("C", 0, "y"), ("A1", 1, "rq"),
)


def build(nc, x, time_row, w1, w2, consts, small, spread, out):
    with ExitStack() as ctx:
        def sb(name, shape, dt=F32):
            return ctx.enter_context(nc.sbuf_tensor(name, shape, dt))

        def psum(name, shape, dt=F32):
            return ctx.enter_context(nc.psum_tensor(name, shape, dt))

        def sem(name):
            return ctx.enter_context(nc.semaphore(name))

        cst = sb("cst", [P, C_END])
        ident = cst[:, C_ID:C_ID + P]
        par = sb("par", [P, S_END])
        wobd = par[:, S_WO:S_WO + P]
        gw2 = par[:, S_GW:S_GW + NE]
        gbb = par[:, S_GB:S_GB + NE]
        gam = par[:, S_GAM:S_GAM + D]
        bet = par[:, S_BET:S_BET + D]
        b1T = par[:, S_B1:S_B1 + NE]
        b2s = par[0:NE, S_B2:S_B2 + D]
        cl = par[0:1, S_CLS:S_CLS + D]
        b2c = par[:, S_B2C:S_B2C + NPAIR]
        iota = sb("iota", [P, NE])
        ones = sb("ones", [P, Q])
        spare = sb("spare", [P, 12])
        mhalf = sb("mhalf", [P, NT])
        wf = sb("wf", [P, 4, 2, D])
        wfe = sb("wfe", [P, 3, P])
        wmix = sb("wmix", [P, 3, D])
        grev = sb("grev", [P, KPAD + 1])
        G = sb("G", [P, KPAD + 1])
        w1raw = sb("w1raw", [P, NE, FF])
        w1h = sb("w1h", [P, NE, FF], F32R)
        w1l = sb("w1l", [P, NE, FF], F32R)
        w2s = sb("w2s", [P, NE, D])

        xt = sb("xt", [P, 16, 4 * VARS])
        uv = sb("uv", [P, UT])
        h = sb("h", [P, 2, NT, D])
        xc1, xc2 = sb("xc1", [P, NT, D]), sb("xc2", [P, NT, D])
        sq1, sq2 = sb("sq1", [P, NT, D]), sb("sq2", [P, NT, D])
        st1, st2 = sb("st1", [P, 4, NT]), sb("st2", [P, 4, NT])
        x1 = sb("x1", [P, NT, 2, D])
        XX = sb("XX", [P, TOK + 1])
        kt = sb("kt", [P, NT, D])
        kv = sb("kv", [P, 2, NT, D])
        kc = sb("kc", [P, Q])
        sk = sb("sk", [P, 2, Q])
        kinit = sb("kinit", [P, 2])
        er = sb("er", [P, Q])
        rq = sb("rq", [P, Q])
        C0 = sb("C0", [P, 2, Q])
        wsum = sb("wsum", [P, Q])
        rw = sb("rw", [P, Q])
        h1 = sb("h1", [P, NT, D])
        h1b = sb("h1b", [P, 2, NT, D])
        x2s = sb("x2s", [P, 2, NT, 2, D])
        xs = sb("xs", [P, 2, UT], F32R)
        lg = sb("lg", [P, NT, NE])
        top8 = sb("top8", [P, NT, 8])
        idx8 = sb("idx8", [P, NT, 8], U32)
        idxf = sb("idxf", [P, NT, 2])
        gsm = sb("gsm", [P, 4, NT])
        eq1 = sb("eq1", [P, NT, NE])
        eq2 = sb("eq2", [P, NT, NE])
        gw = sb("gw", [P, NE, NT])
        gT = sb("gT", [D, 2, P])
        gbs = sb("gbs", [P, 2, NPAIR, UT])

        hr = sb("hr", [P, 4, UT])
        prod = sb("prod", [P, 2, UT])
        acc = sb("acc", [P, 2, UT])
        y2 = sb("y2", [P, NT, D])
        y3 = sb("y3", [P, NT, D])
        y3c = sb("y3c", [P, NT, D])
        y3q = sb("y3q", [P, NT, D])
        st3 = sb("st3", [P, 4, NT])
        yg = sb("yg", [P, NT, D])
        fo = sb("fo", [P, NT, D])

        clw = sb("clw", [1, 3, D])
        cls4 = sb("cls4", [1, 4, 1])
        x1c = sb("x1c", [1, 2, D])
        XXc = sb("XXc", [P, 1])
        kv0t = sb("kv0t", [1, 2, D])
        k0 = sb("k0", [P, 1])
        c0s = sb("c0s", [P, 4])
        h1c = sb("h1c", [1, D])
        x2c = sb("x2c", [1, 2, D])
        x2cT = sb("x2cT", [P, 1])
        lgc = sb("lgc", [1, 1, NE])
        top8c = sb("top8c", [1, 1, 8])
        idx8c = sb("idx8c", [1, 1, 8], U32)
        idxfc = sb("idxfc", [1, 1, 2])
        gsmc = sb("gsmc", [1, 4, 1])
        eqc = sb("eqc", [1, 2, NE])
        gwc = sb("gwc", [1, 1, NE])
        gTc = sb("gTc", [NE, 1])
        gbc = sb("gbc", [P, NE])
        zc = sb("zc", [P, NE])
        hc = sb("hc", [P, NE])
        y3cl = sb("y3cl", [1, 4, D])

        A0 = psum("A0", [P, UT])
        A1 = psum("A1", [P, UT])
        B0 = psum("B0", [P, UT])
        T0 = psum("T0", [P, UT])
        zb = psum("zb", [P, 2, UT])
        yb = psum("yb", [P, 2, UT])

        (l_cst, l_par, l_G, l_w1, l_w2, l_x, l_gate_lo, l_gate_hi) = [
            sem("loaded_" + n) for n in ("consts", "params", "timew", "w1", "w2", "x", "gates_lo", "gates_hi")]
        zeroed, ones_ok = sem("zeroed"), sem("ones_ok")
        fold_ps, wf_ok, wfe_ok = sem("fold_ps"), sem("wf_ok"), sem("wfe_ok")
        mixf_ok, wmix_ok, G_ok = sem("mixf_ok"), sem("wmix_ok"), sem("G_ok")
        w1h_ok, w1l_ok = sem("w1h_ok"), sem("w1l_ok")
        uv_ps, u_done, v_done, h_ps, hu_done, h_done = [
            sem(n) for n in ("uv_ps", "u_done", "v_done", "h_ps", "hu_done", "h_done")]
        x1_ps, xx_lo, xx_hi = sem("x1_ps"), sem("xx_lo"), sem("xx_hi")
        kv_ps, kt_clip, kt_exp, kv_done = [sem(n) for n in ("kv_ps", "kt_clip", "kt_exp", "kv_done")]
        kr_ps, kc_clip, kc_exp, er_done = [sem(n) for n in ("kr_ps", "kc_clip", "kc_exp", "er_done")]
        carry_ps, kinit_ok, sk_done, q_done, rq_done = [
            sem(n) for n in ("carry_ps", "kinit_ok", "sk_done", "q_done", "rq_done")]
        wkv_ps, wsum_done, rw_done, att_ps, h1_done = [
            sem(n) for n in ("wkv_ps", "wsum_done", "rw_done", "att_ps", "h1_done")]
        x2_ps, xs_hi, xs_lo = [sem(n) for n in ("x2_ps", "xs_hi", "xs_lo")]
        lg_ps, lg_done, top_done, idx_done = [sem(n) for n in ("lg_ps", "lg_done", "top_done", "idx_done")]
        idxf_done, gap_done, gexp, gden, g1_done, g2_done = [
            sem(n) for n in ("idxf_done", "gap_done", "gexp", "gden", "g1_done", "g2_done")]
        eq_done, eqg_done, gw_done = sem("eq_done"), sem("eqg_done"), sem("gw_done")
        gT_ps, gT_done, gT_stored, h1b_done = [sem(n) for n in ("gT_ps", "gT_done", "gT_stored", "h1b_done")]
        z_ps, relu_done, h_used = [sem(n) for n in ("z_ps", "relu_done", "h_used")]
        gated, prod_used, acc_done = [sem(n) for n in ("gated", "prod_used", "acc_done")]
        moe_ps, y2_done, moe_read = sem("moe_ps"), sem("y2_done"), sem("moe_read")
        settled = sem("settled")
        yg_done, fo_done, stored = sem("yg_done"), sem("fo_done"), sem("stored")

        def ln_sems(tag):
            return {n: sem(f"{tag}_{n}") for n in ("sum", "center", "square", "sumsq", "var", "rstd", "out")}

        ln1, ln2, ln3, lnc = ln_sems("ln1"), ln_sems("ln2"), ln_sems("ln3"), ln_sems("lnc")
        c_xT, c_xx, c_kv, c_clip, c_exp, c_kv0, c_C0, c_C0sb, c_q, c_rw, c_att, c_h1, c_x2T, c_x2sb, c_lg = [
            sem("cls_" + n) for n in ("xT", "xx", "kv", "clip", "exp", "kv0", "C0", "C0sb", "q", "rw", "att", "h1",
                                      "x2T", "x2sb", "lg")]
        c_gate, c_gexp, c_g, c_gT, c_gTsb, c_z, c_zb, c_h, c_moe, c_y, c_fin, c_fo, c_out = [
            sem("cls_" + n) for n in ("gate", "gexp", "g", "gT", "gTsb", "z", "zb", "h", "moe", "y", "fin", "fo",
                                      "out")]

        uv_v = uv[:, :].rearrange("p (v n) -> p n v", n=NPATCH)

        def tiles(bank):
            return bank[:, 0:NT * D].rearrange("p (i d) -> p i d", d=D)

        def turned(bank, half):
            return bank[:, :].rearrange("p (i s d) -> p s i d", s=2, d=D)[:, half, :, :]

        def reuse(eng, semaphore, value):
            if not (isinstance(value, int) and value <= 0):
                eng.wait_ge(semaphore, value)

        def settle(eng, semaphore, value):
            eng.wait_ge(semaphore, value)
            eng.sem_inc(settled, 1)

        def fill(a1, a2, cls):
            for step in FILL:
                if step[0] == "C":
                    cls(step[2])
                else:
                    (a1 if step[0] == "A1" else a2)(step[1], step[1], step[2])

        def run(a1, a2, m, cls, u, c, with_a1, with_a2):
            for stage, step, *pair in WINDOW:
                if stage == "A1" and with_a1:
                    a1(u + 2, c, step)
                elif stage == "A2" and with_a2:
                    a2(u + 1, 1 - c, step)
                elif stage == "M" and pair == [NPAIR]:
                    if with_a2:
                        m(u + 1, 1 - c, step, 0)
                elif stage == "M":
                    m(u, c, step, pair[0] if pair else None)
                elif stage == "C" and not with_a2:
                    cls(step)

        def windows(eng, a1, a2, m, cls):
            with eng.Fori(0, NB - 1) as b:
                run(a1, a2, m, cls, 2 * b, 0, True, True)
                run(a1, a2, m, cls, 2 * b + 1, 1, True, True)
            run(a1, a2, m, cls, NU - 2, 0, False, True)
            run(a1, a2, m, cls, NU - 1, 1, False, False)

        def ln_center(dve, s, n, src, st, dst, p, t):
            dve.tensor_reduce(st[0:p, 0, :], src, AX_X, ALU.add).then_inc(s["sum"], 1)
            dve.wait_ge(s["sum"], n + 1)
            mean = st[0:p, 0, :].unsqueeze(2).broadcast_to([p, t, D])
            dve.scalar_tensor_tensor(dst, mean, -1.0 / D, src, ALU.mult, ALU.add).then_inc(s["center"], 1)

        def ln_square(act, s, n, src, dst):
            act.wait_ge(s["center"], n + 1)
            act.activation(dst, src, ACT.Square).then_inc(s["square"], 1)

        def ln_var(dve, s, n, sqr, st, p):
            dve.wait_ge(s["square"], n + 1)
            dve.tensor_reduce(st[0:p, 1, :], sqr, AX_X, ALU.add).then_inc(s["sumsq"], 1)
            dve.wait_ge(s["sumsq"], n + 1)
            dve.tensor_scalar(st[0:p, 2, :], st[0:p, 1, :], 1.0 / D, EPS, ALU.mult, ALU.add).then_inc(s["var"], 1)

        def ln_rstd(pool, s, n, st, p, t):
            pool.wait_ge(s["var"], n + 1)
            pool.tensor_tensor(st[0:p, 3, :], st[0:p, 2, :], mhalf[0:p, 0:t], ALU.pow).then_inc(s["rstd"], 1)

        def ln_scale(dve, s, n, src, st, dsts, p, t):
            dve.wait_ge(s["rstd"], n + 1)
            r = st[0:p, 3, :].unsqueeze(2).broadcast_to([p, t, D])
            for dst in dsts:
                last = dve.tensor_tensor(dst, src, r, ALU.mult)
            last.then_inc(s["out"], 1)

        block = ctx.enter_context(nc.Block())

        @block.sync
        def _(sp):
            def load_x(b):
                for half in range(2):
                    src = x[b].rearrange("c (m h q) v -> h c m (q v)", h=2, q=4)[half]
                    sp.dma_start(xt[D * half:D * half + D, :, :], src).then_inc(l_x, 16)

            def spread_gates(u, c):
                sp.wait_ge(gT_done, u + 1)
                sp.dma_start(spread[c], gT[:, c, :]).then_inc(gT_stored, 16)
                sp.wait_ge(gT_stored, 16 * u + 32)
                half = NPAIR // 2
                for part in range(2):
                    for k in range(2):
                        offset = (c * NE + NPAIR * part + k) * UT
                        src = bass.AP(spread.tensor, offset, [[0, D], [2 * UT, half], [1, UT]])
                        sp.dma_start(gbs[D * k:D * k + D, c, half * part:half * part + half, :],
                                     src).then_inc((l_gate_lo, l_gate_hi)[part], 16)

            def store(u, b, c):
                sp.wait_ge(fo_done, u + 2)
                dst = out[b, 1 + c * UT:1 + (c + 1) * UT, :].rearrange("(i p) d -> p i d", p=P)
                sp.dma_start(dst, fo[:, :, :]).then_inc(stored, 16)

            sp.dma_start(cst[:, :], consts).then_inc(l_cst, 16)
            load_x(0)
            sp.dma_start(par[:, :], small).then_inc(l_par, 16)
            sp.dma_start(grev[:, :], bass.AP(time_row.tensor, 0, [[1, P], [1, KPAD + 1]])).then_inc(l_G, 16)
            sp.dma_start(w1raw[:, :, :], w1).then_inc(l_w1, 16)
            sp.dma_start(w2s[:, :, :], w2).then_inc(l_w2, 16)
            sp.wait_ge(uv_ps, 4)
            load_x(1)
            spread_gates(0, 0)
            with sp.Fori(0, NB - 2) as b:
                spread_gates(2 * b + 1, 1)
                store(2 * b, b, 0)
                sp.wait_ge(uv_ps, 4 * b + 8)
                load_x(b + 2)
                spread_gates(2 * b + 2, 0)
                store(2 * b + 1, b, 1)
            for u in range(NU - 4, NU):
                if u + 1 < NU:
                    spread_gates(u + 1, (u + 1) % 2)
                store(u, u // 2, u % 2)
            sp.wait_ge(c_fo, 1)
            for b in range(NB):
                sp.dma_start(out[b, 0:1, :], y3cl[:, 3, :]).then_inc(c_out, 16)
            sp.wait_ge(stored, 16 * (NU + 1))
            sp.wait_ge(c_out, 16 * NB)

        @block.tensor
        def _(pe):
            mm = pe.matmul

            def turn(bank, src, done):
                for i in range(NT):
                    last = pe.transpose(bank[:, P * i:P * i + P], src[:, i, :, :], ident)
                last.then_inc(done, 1)

            def a1(u, c, step):
                if step == "embed":
                    reuse(pe, kc_clip, u)
                    reuse(pe, er_done, u)
                    if c == 0:
                        pe.wait_ge(l_x, 16 * u + 32)
                    for q in range(4):
                        last = mm(A0[:, :], wf[:, q, :, :], xt[:, :, VARS * q + UV * c:VARS * q + UV * c + UV],
                                  start=q == 0, stop=q == 3)
                    last.then_inc(uv_ps, 1)
                elif step == "edge":
                    reuse(pe, kinit_ok, u)
                    mm(A1[:, 0:UV], wfe[D:P, 0, :], xt[D:P, 15, 3 * VARS + UV * c:3 * VARS + UV * c + UV],
                       start=True, stop=True).then_inc(uv_ps, 1)
                elif step == "tokens":
                    pe.wait_ge(v_done, 2 * u + 2)
                    pe.wait_ge(u_done, u + 1)
                    for i in range(NT):
                        last = pe.transpose(A1[:, P * i:P * i + P], uv[:, P * i:P * i + P], ident)
                    last.then_inc(h_ps, 1)
                elif step == "turn":
                    pe.wait_ge(ln1["out"], u + 1)
                    turn(A0, x1, x1_ps)
                elif step == "kv":
                    pe.wait_ge(xx_lo, u + 1)
                    pe.wait_ge(xx_hi, u + 1)
                    for i in range(NT):
                        t = UT * c + P * i
                        last = mm(A1[:, P * i:P * i + P], XX[:, t:t + P], wmix[:, 0:2, :], start=True, stop=True)
                    last.then_inc(kv_ps, 1)
                elif step == "kr":
                    pe.wait_ge(xx_lo, u + 1)
                    pe.wait_ge(xx_hi, u + 1)
                    for i in range(2):
                        for half in range(2):
                            t = UT * c + Q * half
                            last = mm(A0[D * half:D * half + D, Q * i:Q * i + Q], wmix[:, 1 + i, :], XX[:, t:t + Q],
                                      start=True, stop=True)
                    last.then_inc(kr_ps, 1)
                elif step == "carry":
                    pe.wait_ge(kt_exp, u + 1)
                    pe.wait_ge(kv_done, u + 1)
                    for i in range(2):
                        last = mm(A1[D:P, 0:1], kt[:, i, :], ones[:, 0:1], start=i == 0, stop=i == 1)
                    last.then_inc(carry_ps, 1)

            def a2(u, c, step):
                if step == "wkv":
                    reuse(pe, gT_done, u)
                    pe.wait_ge(kv_done, u + 1)
                    n_src = 4 * c + 4
                    for j in range(n_src):
                        for half in range(2):
                            ahead = 2 * Q * c + Q * half - P * j
                            rows = slice(D * half, D * half + D)
                            n_half = n_src - 2 + 2 * half
                            if ahead >= 0:
                                last = mm(B0[rows, 0:Q], kv[:, j // NT, j % NT, :], G[:, ahead:ahead + Q],
                                          start=j == 0, stop=j == n_half - 1, skip_group_check=True)
                            elif ahead == -P:
                                last = mm(B0[rows, P:Q], kv[:, j // NT, j % NT, :], G[:, 0:P],
                                          start=False, stop=j == n_half - 1, skip_group_check=True)
                    last.then_inc(wkv_ps, 1)
                elif step == "att":
                    pe.wait_ge(rw_done, u + 1)
                    out_tiles = B0[:, 0:NT * D].rearrange("p (s i d) -> p s i d", s=2, i=2)
                    for i in range(2):
                        last = mm(out_tiles[:, :, i, :], rw[:, P * i:P * i + P], wobd, start=True, stop=True)
                    last.then_inc(att_ps, 1)
                elif step == "turn":
                    pe.wait_ge(ln2["out"], u + 1)
                    turn(B0, x2s[:, c, :, :, :], x2_ps)
                elif step == "logits":
                    pe.wait_ge(xs_lo, u + 1)
                    for i in range(NT):
                        last = mm(B0[:, NE * i:NE * i + NE], xs[:, c, P * i:P * i + P].bitcast(F32), gw2,
                                  start=True, stop=True)
                    last.then_inc(lg_ps, 1)
                elif step == "spread":
                    settle(pe, gw_done, u + 1)
                    pe.transpose(B0[0:D, 0:P], gw[:, :, :], ident).then_inc(gT_ps, 1)

            def expert_in(u, c, p):
                for k in range(2):
                    e, n = 2 * p + k, 16 * u + 2 * p + k
                    pe.wait_ge(relu_done, n + 1)
                    mm(zb[:, k, :], w1h[:, e, :], xs[:, c, :], start=True, stop=False)
                    mm(zb[:, k, :], w1l[:, e, :], xs[:, c, :], start=False, stop=True).then_inc(z_ps, 1)

            def expert_out(u, c, p):
                n = NPAIR * u + p
                pe.wait_ge(relu_done, 2 * n + 4)
                pe.wait_ge(gated, n + 1)
                for k in range(2):
                    last = mm(yb[D * k:D * k + D, p % 2, :], w2s[:, 2 * p + k, :], hr[:, 2 * (p % 2) + k, :],
                              start=True, stop=True)
                last.then_inc(h_used, 1)

            def moe_tokens(u, c):
                pe.wait_ge(acc_done, u + 1)
                pe.wait_ge(moe_read, u + 1)
                for i in range(NT):
                    last = pe.transpose(T0[:, P * i:P * i + P], acc[:, c, P * i:P * i + P], ident)
                last.then_inc(moe_ps, 1)

            def cls(step):
                zA, yA, yB = T0[:, :], yb[:, 0, :], yb[:, 1, :]
                if step == "x":
                    pe.wait_ge(l_par, 16)
                    pe.wait_ge(ones_ok, 1)
                    pe.wait_ge(lnc["out"], 1)
                    pe.transpose(yB[:, 0:1], x1c[:, :, :], cst[0:1, C_ID:C_ID + 1]).then_inc(c_xT, 1)
                elif step == "kv":
                    pe.wait_ge(c_xx, 1)
                    pe.wait_ge(wmix_ok, 3)
                    mm(zA[0:1, 0:P], XXc[:, :], wmix[:, 0:2, :], start=True, stop=True)
                    for half in range(2):
                        for j in range(2):
                            last = mm(yA[D * half:D * half + D, j:j + 1], wmix[:, 1 + j, :], XXc[:, :],
                                      start=True, stop=True)
                    last.then_inc(c_kv, 1)
                elif step == "c0":
                    pe.wait_ge(c_kv0, 1)
                    pe.wait_ge(G_ok, 1)
                    for c in range(2):
                        for half in range(2):
                            t = 1 + UT * c + Q * half
                            mm(yB[D * half:D * half + D, Q * c:Q * c + Q], kv0t[:, 0, :], G[0:1, t:t + Q],
                               start=True, stop=True)
                    mm(yA[0:D, 2:3], kv0t[:, 0, :], G[0:1, 0:1], start=True, stop=True).then_inc(c_C0, 1)
                elif step == "att":
                    pe.wait_ge(c_rw, 1)
                    mm(zA[0:1, 0:D], c0s[0:D, 3:4], par[0:D, S_WO:S_WO + D], start=True, stop=True).then_inc(c_att, 1)
                elif step == "edge":
                    pe.wait_ge(wfe_ok, 3)
                elif step == "turn":
                    pe.wait_ge(lnc["out"], 2)
                    pe.wait_ge(c_C0sb, 1)
                    pe.transpose(yB[:, 0:1], x2c[:, :, :], cst[0:1, C_ID:C_ID + 1]).then_inc(c_x2T, 1)
                    pe.wait_ge(c_x2sb, 1)
                    mm(yB[0:1, 0:NE], x2cT[0:D, :], par[0:D, S_GW:S_GW + NE], start=True, stop=True).then_inc(c_lg, 1)
                elif step in ("z0", "z1"):
                    pe.wait_ge(l_w1, 16)
                    for e in range(NPAIR * int(step[1]), NPAIR * int(step[1]) + NPAIR):
                        last = mm(yA[:, e:e + 1], w1raw[0:D, e, :], x2cT[0:D, :], start=True, stop=True)
                    last.then_inc(c_z, 1)
                elif step == "spread":
                    pe.wait_ge(c_g, 4)
                    mm(yB[:, 0:NE], ones[0:1, 0:P], gwc[:, 0, :], start=True, stop=True)
                    pe.transpose(yB[0:NE, NE:NE + 1], gwc[:, 0, :], cst[0:1, C_ID:C_ID + 1]).then_inc(c_gT, 1)
                elif step == "experts":
                    pe.wait_ge(w1l_ok, 1)
                    expert_in(0, 0, 0)
                elif step == "y0":
                    pe.wait_ge(c_gTsb, 1)
                    pe.wait_ge(c_h, 1)
                    pe.wait_ge(l_w2, 16)
                    mm(zA[0:1, 0:D], gTc[:, :], b2s, start=True, stop=False)
                    for e in range(NPAIR):
                        mm(zA[0:1, 0:D], hc[:, e:e + 1], w2s[:, e, :], start=False, stop=False)
                elif step == "y1":
                    for e in range(NPAIR, NE):
                        last = mm(zA[0:1, 0:D], hc[:, e:e + 1], w2s[:, e, :], start=False, stop=e == NE - 1)
                    last.then_inc(c_moe, 1)

            pe.wait_ge(l_cst, 16)
            for g in range(16):
                for half in range(2):
                    last = mm(B0[D * half:D * half + D, 32 * g:32 * g + 32], cst[:, C_TOKW + D * g:C_TOKW + D * g + D],
                              cst[:, C_DFT + 32 * half:C_DFT + 32 * half + 32], start=True, stop=True)
            last.then_inc(fold_ps, 1)
            pe.wait_ge(wf_ok, 2)
            fill(a1, a2, cls)

            def m(u, c, step, p):
                if step == "in":
                    expert_in(u, c, p)
                elif step == "out":
                    expert_out(u, c, p)
                elif step == "tokens":
                    moe_tokens(u, c)

            windows(pe, a1, a2, m, cls)

        @block.scalar
        def _(act):
            fn = act.activation

            def a1(u, c, step):
                if step == "edge":
                    act.wait_ge(uv_ps, 2 * u + 1)
                    fn(uv_v[0:D, :, :], A0[0:D, :].rearrange("p (m v) -> p m v", v=UV), ACT.Copy).then_inc(u_done, 1)
                elif step == "tokens":
                    reuse(act, h1_done, u - 1)
                    act.wait_ge(h_ps, u + 1)
                    fn(h[:, c, :, :], turned(A1, 0), ACT.Copy).then_inc(hu_done, 1)
                elif step == "var":
                    ln_square(act, ln1, u, xc1[:, :, :], sq1[:, :, :])
                elif step == "turn":
                    act.wait_ge(x1_ps, u + 1)
                    fn(XX[0:D, UT * c:UT * c + UT], A0[0:D, :], ACT.Copy).then_inc(xx_lo, 1)
                elif step == "kv":
                    act.wait_ge(kt_clip, u + 1)
                    fn(kt[:, :, :], kt[:, :, :], ACT.Exp).then_inc(kt_exp, 1)
                elif step == "kr":
                    act.wait_ge(kc_clip, u + 1)
                    fn(kc[:, :], kc[:, :], ACT.Exp).then_inc(kc_exp, 1)
                    fn(er[:, :], A0[:, Q:2 * Q], ACT.Exp, scale=-1.0).then_inc(er_done, 1)

            def a2(u, c, step):
                if step == "var":
                    ln_square(act, ln2, u, xc2[:, :, :], sq2[:, :, :])
                elif step == "turn":
                    act.wait_ge(x2_ps, u + 1)
                    fn(xs[:, c, :], B0[:, :], ACT.Copy).then_inc(xs_hi, 1)
                elif step == "gates":
                    act.wait_ge(gap_done, u + 1)
                    fn(gsm[:, 1, :], gsm[:, 0, :], ACT.Exp).then_inc(gexp, 1)
                elif step == "spread":
                    reuse(act, gT_stored, 16 * u)
                    act.wait_ge(gT_ps, u + 1)
                    fn(gT[:, c, :], B0[0:D, 0:P], ACT.Copy).then_inc(gT_done, 1)

            def relu(u, p):
                n = NPAIR * u + p
                act.wait_ge(h_used, n + 1)
                for k in range(2):
                    act.wait_ge(z_ps, 2 * n + k + 1)
                    fn(hr[:, 2 * (p % 2) + k, :], zb[:, k, :], ACT.Relu,
                       bias=b1T[:, 2 * p + k:2 * p + k + 1]).then_inc(relu_done, 1)

            def cls(step):
                zA, yA, yB = T0[:, :], yb[:, 0, :], yb[:, 1, :]
                if step == "x":
                    act.wait_ge(c_xT, 1)
                    fn(XX[D:P, 0:1], yB[D:P, 0:1], ACT.Copy)
                    act.wait_ge(zeroed, 3)
                    fn(XXc[0:D, :], yB[0:D, 0:1], ACT.Copy).then_inc(c_xx, 1)
                elif step == "kv":
                    act.wait_ge(c_clip, 2)
                    fn(kv0t[:, 1, :], kv0t[:, 1, :], ACT.Exp)
                    fn(k0[:, :], k0[:, :], ACT.Exp)
                    fn(c0s[:, 0:1], yA[:, 1:2], ACT.Exp, scale=-1.0).then_inc(c_exp, 1)
                elif step == "c0":
                    act.wait_ge(c_C0, 1)
                    fn(C0[:, :, :], yB.rearrange("p (c t) -> p c t", c=2), ACT.Copy).then_inc(c_C0sb, 1)
                elif step == "norm":
                    ln_square(act, lnc, 1, clw[:, 0:1, :], clw[:, 1:2, :])
                elif step == "turn":
                    act.wait_ge(c_x2T, 1)
                    fn(x2cT[:, :], yB[:, 0:1], ACT.Copy).then_inc(c_x2sb, 1)
                elif step == "gates":
                    act.wait_ge(c_gate, 4)
                    fn(gsmc[:, 1, :], gsmc[:, 0, :], ACT.Exp).then_inc(c_gexp, 1)
                elif step == "w1":
                    act.wait_ge(l_w1, 16)
                    fn(w1h[:, :, :], w1raw[:, :, :], ACT.Copy).then_inc(w1h_ok, 1)
                elif step == "spread":
                    act.wait_ge(c_gT, 1)
                    fn(gTc[:, :], yB[0:NE, NE:NE + 1], ACT.Copy)
                    fn(gbc[:, :], yB[:, 0:NE], ACT.Copy).then_inc(c_gTsb, 1)
                elif step == "experts":
                    relu(0, 0)
                elif step == "out":
                    ln_square(act, lnc, 2, y3cl[:, 1:2, :], y3cl[:, 2:3, :])

            act.wait_ge(fold_ps, 1)
            fn(wf[0:D, :, :, :].rearrange("p q s o -> p (q s) o"), B0[0:D, :].rearrange("p (o j) -> p j o", j=8),
               ACT.Copy).then_inc(wf_ok, 1)
            act.wait_ge(l_par, 16)
            ln_square(act, lnc, 0, clw[:, 0:1, :], clw[:, 1:2, :])
            fill(a1, a2, cls)

            def m(u, c, step, p):
                if step == "in":
                    relu(u, p)
                elif step == "var":
                    ln_square(act, ln3, u, y3c[:, :, :], y3q[:, :, :])

            windows(act, a1, a2, m, cls)

        @block.vector
        def _(dve):
            tt, ts, stt = dve.tensor_tensor, dve.tensor_scalar, dve.scalar_tensor_tensor

            def gate_top(lgt, top, idx, n_tiles, n0, s_top, s_idx):
                for i in range(n_tiles):
                    dve.max(top[:, i, :], lgt[:, i, :]).then_inc(s_top, 1)
                for i in range(n_tiles):
                    settle(dve, s_top, n0 + i + 1)
                    dve.max_index(idx[:, i, :], top[:, i, :], lgt[:, i, :]).then_inc(s_idx, 1)

            def a1(u, c, step):
                if step == "edge":
                    dve.wait_ge(uv_ps, 2 * u + 1)
                    dve.tensor_copy(uv_v[D:P, 0:15, :],
                                    A0[D:P, UV:].rearrange("p (m v) -> p m v", v=UV)).then_inc(v_done, 1)
                    dve.wait_ge(uv_ps, 2 * u + 2)
                    dve.tensor_copy(uv_v[D:P, 15, :], A1[D:P, 0:UV]).then_inc(v_done, 1)
                elif step == "tokens":
                    dve.wait_ge(hu_done, u + 1)
                    tt(h[:, c, :, :], turned(A1, 1), h[:, c, :, :], ALU.add).then_inc(h_done, 1)
                    dve.wait_ge(h_done, u + 1)
                    ln_center(dve, ln1, u, h[:, c, :, :], st1, xc1[:, :, :], P, NT)
                elif step == "var":
                    ln_var(dve, ln1, u, sq1[:, :, :], st1, P)
                elif step == "scale":
                    ln_scale(dve, ln1, u, xc1[:, :, :], st1, [x1[:, :, 0, :], x1[:, :, 1, :]], P, NT)
                elif step == "turn":
                    dve.wait_ge(x1_ps, u + 1)
                    dve.tensor_copy(XX[D:P, 1 + UT * c:1 + UT * c + UT], A0[D:P, :]).then_inc(xx_hi, 1)
                elif step == "kv":
                    bank = A1[:, :].rearrange("p (i w d) -> p i w d", i=NT, w=2)
                    dve.wait_ge(kv_ps, u + 1)
                    ts(kt[:, :, :], bank[:, :, 1, :], -60.0, 30.0, ALU.max, ALU.min).then_inc(kt_clip, 1)
                    dve.wait_ge(kt_exp, u + 1)
                    tt(kv[:, c, :, :], kt[:, :, :], bank[:, :, 0, :], ALU.mult).then_inc(kv_done, 1)
                elif step == "kr":
                    dve.wait_ge(kr_ps, u + 1)
                    ts(kc[:, :], A0[:, 0:Q], -60.0, 30.0, ALU.max, ALU.min).then_inc(kc_clip, 1)
                elif step == "carry":
                    dve.wait_ge(carry_ps, u + 1)
                    before = k0[D:P, :] if c == 0 else sk[D:P, 0, Q - 1:Q]
                    if c == 1:
                        dve.tensor_copy(kinit[0:D, 1:2], sk[D:P, 0, Q - 1:Q])
                    tt(kinit[D:P, c:c + 1], A1[D:P, 0:1], before, ALU.add).then_inc(kinit_ok, 1)
                    dve.wait_ge(kinit_ok, u + 1)
                    dve.wait_ge(kc_exp, u + 1)
                    dve.tensor_tensor_scan(sk[:, c, :], ones[:, :], kc[:, :], kinit[:, c:c + 1], ALU.mult,
                                           ALU.add).then_inc(sk_done, 1)
                    dve.wait_ge(sk_done, u + 1)
                    dve.wait_ge(er_done, u + 1)
                    stt(er[:, :], er[:, :], 1.0, sk[:, c, :], ALU.add, ALU.mult).then_inc(q_done, 1)
                elif step == "rq":
                    dve.wait_ge(q_done, u + 1)
                    dve.reciprocal(rq[:, :], er[:, :]).then_inc(rq_done, 1)

            def a2(u, c, step):
                if step == "wkv":
                    dve.wait_ge(wkv_ps, u + 1)
                    tt(wsum[:, :], B0[:, 0:Q], C0[:, c, :], ALU.add).then_inc(wsum_done, 1)
                    dve.wait_ge(wsum_done, u + 1)
                    dve.wait_ge(rq_done, u + 1)
                    tt(rw[:, :], wsum[:, :], rq[:, :], ALU.mult).then_inc(rw_done, 1)
                elif step == "att":
                    reuse(dve, h1b_done, u)
                    dve.wait_ge(att_ps, u + 1)
                    tt(h1[:, :, :], tiles(B0), h[:, c, :, :], ALU.add).then_inc(h1_done, 1)
                    settle(dve, h1_done, u + 1)
                    ln_center(dve, ln2, u, h1[:, :, :], st2, xc2[:, :, :], P, NT)
                elif step == "var":
                    ln_var(dve, ln2, u, sq2[:, :, :], st2, P)
                elif step == "scale":
                    ln_scale(dve, ln2, u, xc2[:, :, :], st2, [x2s[:, c, :, 0, :], x2s[:, c, :, 1, :]], P, NT)
                elif step == "turn":
                    lo = xs[D:P, c, :]
                    dve.wait_ge(xs_hi, u + 1)
                    tt(lo, B0[D:P, :], lo.bitcast(F32), ALU.subtract).then_inc(xs_lo, 1)
                elif step == "logits":
                    dve.wait_ge(lg_ps, u + 1)
                    tt(lg[:, :, :], B0[:, 0:NT * NE].rearrange("p (i e) -> p i e", e=NE),
                       gbb.unsqueeze(1).broadcast_to([P, NT, NE]), ALU.add).then_inc(lg_done, 1)
                    settle(dve, lg_done, u + 1)
                    gate_top(lg, top8, idx8, NT, NT * u, top_done, idx_done)
                    tt(gsm[:, 0, :], top8[:, :, 1], top8[:, :, 0], ALU.subtract).then_inc(gap_done, 1)
                    dve.wait_ge(idx_done, NT * u + NT)
                    dve.tensor_copy(idxf[:, :, :], idx8[:, :, 0:2]).then_inc(idxf_done, 1)
                elif step == "gates":
                    dve.wait_ge(idxf_done, u + 1)
                    for k, row in enumerate((eq1, eq2)):
                        tt(row[:, :, :], iota[:, :].unsqueeze(1).broadcast_to([P, NT, NE]),
                           idxf[:, :, k:k + 1].broadcast_to([P, NT, NE]), ALU.is_equal).then_inc(eq_done, 1)
                    dve.wait_ge(gexp, u + 1)
                    ts(gsm[:, 2, :], gsm[:, 1, :], 1.0, None, ALU.add).then_inc(gden, 1)
                    dve.wait_ge(gden, u + 1)
                    dve.reciprocal(gsm[:, 3, :], gsm[:, 2, :]).then_inc(g1_done, 1)
                    dve.wait_ge(g1_done, u + 1)
                    tt(gsm[:, 2, :], gsm[:, 1, :], gsm[:, 3, :], ALU.mult).then_inc(g2_done, 1)
                    dve.wait_ge(eq_done, 2 * u + 2)
                    dve.wait_ge(g2_done, u + 1)
                    for row, w in ((eq1, gsm[:, 3, :]), (eq2, gsm[:, 2, :])):
                        last = tt(row[:, :, :], row[:, :, :], w.unsqueeze(2).broadcast_to([P, NT, NE]), ALU.mult)
                    last.then_inc(eqg_done, 1)
                    dve.wait_ge(eqg_done, u + 1)
                    tt(gw[:, :, :].rearrange("p e i -> p i e"), eq1[:, :, :], eq2[:, :, :], ALU.add).then_inc(gw_done, 1)

            def gate(u, c, p):
                n = NPAIR * u + p
                dve.wait_ge(h_used, n + 3)
                if p == 0:
                    dve.wait_ge(l_gate_lo, 32 * u + 32)
                    dve.wait_ge(moe_ps, u + 1)
                if p == NPAIR // 2:
                    dve.wait_ge(l_gate_hi, 32 * u + 32)
                if p > 1:
                    dve.wait_ge(prod_used, (NPAIR - 2) * u + p)
                dst = acc[:, c, :] if p == 0 else prod[:, p % 2, :]
                stt(dst, yb[:, p % 2, :], b2c[:, p:p + 1], gbs[:, c, p, :], ALU.add, ALU.mult).then_inc(gated, 1)
                if p == NPAIR - 1:
                    dve.wait_ge(gated, n + 3)
                    dve.wait_ge(prod_used, (NPAIR - 2) * u + NPAIR)
                    tt(acc[:, c, :], acc[:, c, :], prod[:, p % 2, :], ALU.add).then_inc(acc_done, 1)


            def cls(step):
                zA, yA, yB = T0[:, :], yb[:, 0, :], yb[:, 1, :]
                if step == "kv":
                    dve.wait_ge(c_kv, 1)
                    ts(kv0t[:, 1, :], zA[0:1, D:P], -60.0, 30.0, ALU.max, ALU.min).then_inc(c_clip, 1)
                    ts(k0[:, :], yA[:, 0:1], -60.0, 30.0, ALU.max, ALU.min).then_inc(c_clip, 1)
                    dve.wait_ge(c_exp, 1)
                    tt(kv0t[:, 0, :], kv0t[:, 1, :], zA[0:1, 0:D], ALU.mult).then_inc(c_kv0, 1)
                    dve.tensor_copy(kinit[0:D, 0:1], k0[0:D, :])
                    stt(c0s[:, 1:2], c0s[:, 0:1], 1.0, k0[:, :], ALU.add, ALU.mult).then_inc(c_q, 1)
                    dve.wait_ge(c_q, 1)
                    dve.reciprocal(c0s[:, 2:3], c0s[:, 1:2]).then_inc(c_q, 1)
                elif step == "edge":
                    dve.wait_ge(wf_ok, 2)
                    dve.tensor_reduce(wfe[:, 1, :], wf[:, :, :, :].rearrange("p q s o -> p (s o) q"), AX_X,
                                      ALU.add).then_inc(wfe_ok, 1)
                    dve.wait_ge(wfe_ok, 1)
                    dve.tensor_copy(wfe[D:P, 2, :], wfe[0:D, 1, :]).then_inc(wfe_ok, 1)
                    dve.wait_ge(wfe_ok, 2)
                    tt(wfe[D:P, 0, :], wfe[D:P, 1, :], wfe[D:P, 2, :], ALU.add).then_inc(wfe_ok, 1)
                elif step == "c0":
                    dve.wait_ge(c_q, 2)
                    dve.wait_ge(c_C0, 1)
                    tt(c0s[0:D, 3:4], yA[0:D, 2:3], c0s[0:D, 2:3], ALU.mult).then_inc(c_rw, 1)
                elif step == "att":
                    dve.wait_ge(c_att, 1)
                    tt(h1c[:, :], zA[0:1, 0:D], cl, ALU.add).then_inc(c_h1, 1)
                elif step == "norm":
                    dve.wait_ge(c_h1, 1)
                    ln_center(dve, lnc, 1, h1c[:, :].unsqueeze(1), cls4, clw[:, 0:1, :], 1, 1)
                    ln_var(dve, lnc, 1, clw[:, 1:2, :], cls4, 1)
                    ln_scale(dve, lnc, 1, clw[:, 0:1, :], cls4, [x2c[:, 0:1, :], x2c[:, 1:2, :]], 1, 1)
                elif step == "gates":
                    dve.wait_ge(c_lg, 1)
                    tt(lgc[:, 0, :], yB[0:1, 0:NE], par[0:1, S_GB:S_GB + NE], ALU.add).then_inc(c_gate, 1)
                    dve.wait_ge(c_gate, 1)
                    gate_top(lgc, top8c, idx8c, 1, 1, c_gate, c_gate)
                    tt(gsmc[:, 0, :], top8c[:, :, 1], top8c[:, :, 0], ALU.subtract).then_inc(c_gate, 1)
                    dve.wait_ge(c_gate, 4)
                    dve.tensor_copy(idxfc[:, :, :], idx8c[:, :, 0:2]).then_inc(c_gate, 1)
                    dve.wait_ge(c_gate, 5)
                    for k in range(2):
                        ts(eqc[:, k, :], iota[0:1, :], idxfc[:, 0, k:k + 1], None, ALU.is_equal)
                    dve.wait_ge(c_gexp, 1)
                    ts(gsmc[:, 2, :], gsmc[:, 1, :], 1.0, None, ALU.add).then_inc(c_g, 1)
                    dve.wait_ge(c_g, 1)
                    dve.reciprocal(gsmc[:, 3, :], gsmc[:, 2, :]).then_inc(c_g, 1)
                    dve.wait_ge(c_g, 2)
                    tt(gsmc[:, 2, :], gsmc[:, 1, :], gsmc[:, 3, :], ALU.mult)
                    ts(gwc[:, 0, :], eqc[:, 0, :], gsmc[:, 3, :], None, ALU.mult).then_inc(c_g, 1)
                    dve.wait_ge(c_g, 3)
                    stt(gwc[:, 0, :], eqc[:, 1, :], gsmc[:, 2, :], gwc[:, 0, :], ALU.mult, ALU.add).then_inc(c_g, 1)
                elif step == "spread":
                    dve.wait_ge(c_z, 2)
                    tt(zc[:, :], yA[:, 0:NE], b1T, ALU.add).then_inc(c_zb, 1)
                    dve.wait_ge(c_zb, 1)
                    dve.wait_ge(c_gTsb, 1)
                    stt(hc[:, :], zc[:, :], 0.0, gbc[:, :], ALU.max, ALU.mult).then_inc(c_h, 1)
                elif step == "y":
                    dve.wait_ge(c_moe, 1)
                    tt(y3cl[:, 0, :], zA[0:1, 0:D], x2c[:, 0, :], ALU.add).then_inc(c_y, 1)
                elif step == "out":
                    dve.wait_ge(c_y, 1)
                    ln_center(dve, lnc, 2, y3cl[:, 0:1, :], cls4, y3cl[:, 1:2, :], 1, 1)
                    ln_var(dve, lnc, 2, y3cl[:, 2:3, :], cls4, 1)
                    ln_scale(dve, lnc, 2, y3cl[:, 1:2, :], cls4, [y3cl[:, 0:1, :]], 1, 1)
                    dve.wait_ge(lnc["out"], 3)
                    tt(y3cl[:, 1, :], y3cl[:, 0, :], par[0:1, S_GAM:S_GAM + D], ALU.mult).then_inc(c_fin, 1)
                    dve.wait_ge(c_fin, 1)
                    tt(y3cl[:, 2, :], y3cl[:, 1, :], par[0:1, S_BET:S_BET + D], ALU.add).then_inc(c_fin, 1)
                    dve.wait_ge(c_fin, 2)
                    tt(y3cl[:, 3, :], y3cl[:, 2, :], h1c[:, :], ALU.add).then_inc(c_fo, 1)

            dve.memset(ones[:, :], 1.0).then_inc(ones_ok, 1)
            dve.wait_ge(fold_ps, 1)
            dve.tensor_copy(wf[D:P, :, :, :].rearrange("p q s o -> p (q s) o"),
                            B0[D:P, :].rearrange("p (o j) -> p j o", j=8)).then_inc(wf_ok, 1)
            dve.wait_ge(l_par, 16)
            mix_hi = par[D:P, S_MIX:S_MIX + 3]
            ts(mix_hi, mix_hi, -1.0, 1.0, ALU.mult, ALU.add).then_inc(mixf_ok, 1)
            ln_center(dve, lnc, 0, cl.unsqueeze(1), cls4, clw[:, 0:1, :], 1, 1)
            dve.wait_ge(mixf_ok, 1)
            for i in range(3):
                ts(wmix[:, i, :], par[:, S_W + D * i:S_W + D * i + D], par[:, S_MIX + i:S_MIX + i + 1], None,
                   ALU.mult).then_inc(wmix_ok, 1)
            ln_var(dve, lnc, 0, clw[:, 1:2, :], cls4, 1)
            ln_scale(dve, lnc, 0, clw[:, 0:1, :], cls4, [x1c[:, 0:1, :], x1c[:, 1:2, :]], 1, 1)
            dve.wait_ge(zeroed, 3)
            dve.wait_ge(l_G, 16)
            dve.tensor_copy(G[:, :], grev[:, ::-1]).then_inc(G_ok, 1)
            fill(a1, a2, cls)

            def m(u, c, step, p):
                if step == "out":
                    gate(u, c, p)
                elif step == "center":
                    dve.wait_ge(moe_ps, u + 3)
                    tt(y2[:, :, :], turned(T0, 0), x2s[:, c, :, 0, :], ALU.add).then_inc(y2_done, 1)
                    dve.wait_ge(y2_done, u + 1)
                    tt(y3[:, :, :], turned(T0, 1), y2[:, :, :], ALU.add).then_inc(moe_read, 1)
                    dve.wait_ge(moe_read, u + 2)
                    ln_center(dve, ln3, u, y3[:, :, :], st3, y3c[:, :, :], P, NT)
                elif step == "var":
                    ln_var(dve, ln3, u, y3q[:, :, :], st3, P)
                elif step == "scale":
                    dve.wait_ge(ln3["rstd"], u + 1)
                    for i in range(NT):
                        last = stt(yg[:, i, :], y3c[:, i, :], st3[:, 3, i:i + 1], gam, ALU.mult, ALU.mult)
                    last.then_inc(yg_done, 1)
                    dve.wait_ge(yg_done, u + 1)
                    dve.wait_ge(h1b_done, u + 1)
                    dve.wait_ge(stored, 16 * u + 16)
                    tt(fo[:, :, :], yg[:, :, :], h1b[:, c, :, :], ALU.add).then_inc(fo_done, 1)

            windows(dve, a1, a2, m, cls)

        @block.gpsimd
        def _(pool):
            def a1(u, c, step):
                if step == "var":
                    ln_rstd(pool, ln1, u, st1, P, NT)

            def a2(u, c, step):
                if step == "var":
                    ln_rstd(pool, ln2, u, st2, P, NT)
                    reuse(pool, fo_done, u)
                    pool.tensor_tensor(h1b[:, c, :, :], h1[:, :, :], bet.unsqueeze(1).broadcast_to([P, NT, D]),
                                       ALU.add).then_inc(h1b_done, 1)

            def add_pair(u, c, p):
                n = NPAIR * u + p
                pool.wait_ge(gated, n + 3)
                pool.wait_ge(prod_used, (NPAIR - 2) * u + p + 1)
                pool.tensor_tensor(acc[:, c, :], acc[:, c, :], prod[:, p % 2, :], ALU.add).then_inc(prod_used, 1)

            def cls(step):
                if step == "norm":
                    ln_rstd(pool, lnc, 1, cls4, 1, 1)
                elif step == "w1":
                    pool.wait_ge(w1h_ok, 1)
                    pool.tensor_tensor(w1l[:, :, :], w1raw[:, :, :], w1h[:, :, :].bitcast(F32),
                                       ALU.subtract).then_inc(w1l_ok, 1)
                elif step == "out":
                    ln_rstd(pool, lnc, 2, cls4, 1, 1)

            for i, (counter, free) in enumerate(((relu_done, 2), (gated, 2), (h_used, 2), (prod_used, 2), (moe_ps, 2),
                                                 (moe_read, 1), (stored, 16), (fo_done, 1), (gT_stored, 16))):
                pool.memset(spare[:, i:i + 1], 0.0).then_inc(counter, free)
            pool.memset(mhalf[:, :], -0.5).then_inc(zeroed, 1)
            pool.memset(XXc[:, :], 0.0).then_inc(zeroed, 1)
            pool.iota(iota[:, :], [[1, NE]], base=0, channel_multiplier=0,
                      allow_small_or_imprecise_dtypes=True).then_inc(zeroed, 1)
            pool.wait_ge(zeroed, 3)
            ln_rstd(pool, lnc, 0, cls4, 1, 1)
            pool.wait_ge(l_par, 16)
            fill(a1, a2, cls)

            def m(u, c, step, p):
                if step == "out" and 0 < p < NPAIR - 1:
                    add_pair(u, c, p)
                elif step == "var":
                    ln_rstd(pool, ln3, u, st3, P, NT)

            windows(pool, a1, a2, m, cls)


def _consts(np, tok_W):
    c = np.zeros((P, C_END), np.float32)
    c[:, C_ID:C_ID + P] = np.eye(P)
    angle = 2 * np.pi * np.arange(9)[:, None] * np.arange(16)[None, :] / 16
    dft = np.concatenate([np.cos(angle), -np.sin(angle)]) / 4
    for g in range(4):
        rows = slice(32 * g, 32 * g + 18)
        for half in range(2):
            t = C_DFT + 32 * half + 8 * g
            c[rows, t:t + 8] = dft.reshape(18, 2, 2, 4)[:, :, half].transpose(0, 2, 1).reshape(18, 8)
        c[rows, C_TOKW:] = tok_W.reshape(16, 4, 18, D)[:, g].transpose(1, 0, 2).reshape(18, 16 * D)
    return c


def _small(np, a):
    s = np.zeros((P, S_END), np.float32)
    for i, n in enumerate("vkr"):
        s[:, S_W + D * i:S_W + D * i + D] = np.tile(a[f"L0_attn_W{n}"], (2, 1))
        s[:, S_MIX + i] = np.tile(a[f"L0_attn_time_mix_{n}"].reshape(D), 2)
    for half in range(2):
        s[D * half:D * half + D, S_WO + D * half:S_WO + D * half + D] = a["L0_attn_Wo"]
    s[:, S_GW:S_GW + NE] = np.tile(a["L0_ffn_gate_w"], (2, 1))
    s[:, S_GB:S_GB + NE] = a["L0_ffn_gate_b"]
    s[:, S_GAM:S_GAM + D] = a["L0_ffn_gamma"]
    s[:, S_BET:S_BET + D] = a["L0_ffn_beta"]
    s[:, S_B1:S_B1 + NE] = a["L0_ffn_b1"].T
    s[0:NE, S_B2:S_B2 + D] = a["L0_ffn_b2"]
    s[0, S_CLS:S_CLS + D] = a["cls_tok"].reshape(D)
    s[:, S_B2C:S_B2C + NPAIR] = a["L0_ffn_b2"].reshape(NPAIR, P).T
    return s


def kernel(**inputs):
    import numpy as _np
    import concourse.bacc as _bacc
    from concourse.bass_utils import run_bass_kernel_spmd as _run

    a = {name: _np.asarray(v) for name, v in inputs.items()}
    time_w = a["L0_attn_time_w"]
    row = _np.concatenate([_np.repeat(time_w[0:1], KPAD + 1 - WLEN), time_w, _np.zeros(P, _np.float32)])
    arrays = {
        "in_x": a["x"],
        "in_time_row": row,
        "in_w1": _np.tile(a["L0_ffn_w1"].transpose(1, 0, 2), (2, 1, 1)),
        "in_w2": a["L0_ffn_w2"].transpose(1, 0, 2),
        "in_consts": _consts(_np, a["L0_tok_W"]),
        "in_small": _small(_np, a),
    }
    arrays = {name: _np.ascontiguousarray(v) for name, v in arrays.items()}
    nc = _bacc.Bacc("TRN2", target_bir_lowering=False, num_devices=1)
    args = [nc.dram_tensor(name, v.shape, mybir.dt.from_np(v.dtype), kind="ExternalInput").ap()
            for name, v in arrays.items()]
    args.append(nc.dram_tensor("router_weights", (2, D, P), F32, kind="Internal").ap())
    args.append(nc.dram_tensor("out_tokens", (NB, TOK + 1, D), F32, kind="ExternalOutput").ap())
    build(nc, *args)
    r = _run(nc, [arrays], core_ids=[0])
    return r.results[0]["out_tokens"]
```
